# Optimizing a Trainium2 kernel written in Bass

```python
import numpy as np
import jax
import jax.numpy as jnp

def _softmax(x, axis=-1):
    return jax.nn.softmax(x, axis=axis)

def _gelu(x):
    return jax.nn.gelu(x, approximate=True)

def _silu(x):
    return jax.nn.silu(x)

def _sigmoid(x):
    return jax.nn.sigmoid(x)

def _layernorm(x, axis=-1, eps=1e-05):
    m = jnp.mean(x, axis=axis, keepdims=True)
    v = jnp.var(x, axis=axis, keepdims=True)
    return (x - m) / jnp.sqrt(v + eps)

def _scatter_add(tgt, idx, src, axis=0):
    return tgt.at[idx].add(src)

def _segment_sum(src, seg, n):
    return jax.ops.segment_sum(src, seg, n)
kernel_name = 'mk_lm_tower_d1_tok_ids512_r4_d8398d'

def setup_inputs(seed: int=0):
    np.random.seed(seed)
    _w = jnp.asarray

    def _rec_inputs():
        import jax
        import jax.numpy as jnp
        _rk = jax.random.key(seed)
        x = jax.random.randint(jax.random.fold_in(_rk, 1), (8, 512), 0, 33, jnp.int32)
        return x
    x = _rec_inputs()

    def _L0_tok_setup():
        import jax, jax.numpy as jnp
        import numpy as np
        B, S, H, L, V, PAD = (32, 256, 128, 8, 33, 1)

        def layer_norm(x, g, b, eps):
            mu = jnp.mean(x, axis=-1, keepdims=True)
            var = jnp.mean(jnp.square(x - mu), axis=-1, keepdims=True)
            return (x - mu) * jax.lax.rsqrt(var + eps) * g + b

        def conv1d_same(x, w):
            return jax.lax.conv_general_dilated(x, w, window_strides=(1,), padding=[(1, 1)], dimension_numbers=('NWC', 'WIO', 'NWC'))
        key = jax.random.key(seed)
        ks = jax.random.split(key, 4)
        tokens = jax.random.randint(ks[0], (B, S), 0, V)
        emb = jax.random.normal(ks[1], (V, H), dtype=jnp.float32) * 0.02
        W1 = jax.random.normal(ks[2], (L, 3, H, H), dtype=jnp.float32) * (2.0 / (3 * H)) ** 0.5
        W2 = jax.random.normal(ks[3], (L, 3, H, H), dtype=jnp.float32) * (2.0 / (3 * H)) ** 0.5
        return {'tokens': tokens, 'emb': emb, 'ln0_g': jnp.ones((H,), jnp.float32), 'ln0_b': jnp.zeros((H,), jnp.float32), 'W1': W1, 'g1': jnp.ones((L, H), jnp.float32), 'b1': jnp.zeros((L, H), jnp.float32), 'W2': W2, 'g2': jnp.ones((L, H), jnp.float32), 'b2': jnp.zeros((L, H), jnp.float32)}
    _L0_tok_all = _L0_tok_setup()
    _L0_tok_in = {k: v for k, v in _L0_tok_all.items() if k in ('emb', 'ln0_g', 'ln0_b', 'W1', 'g1', 'b1', 'W2', 'g2', 'b2')}
    del _L0_tok_all

    def _L0_attn_setup():
        import jax, jax.numpy as jnp
        import numpy as np
        DIM = 128
        HEADS = 8
        DIM_HEAD = 64
        DIM_INNER = HEADS * DIM_HEAD
        FRAC_GRAD = 0.5
        SCALE = DIM_HEAD ** (-0.5)
        EPS_CUMPROD = 1e-10
        EPS_INV = 1e-08

        def _rms_norm(x, gamma):
            nrm = jnp.linalg.norm(x, axis=-1, keepdims=True)
            return x / jnp.maximum(nrm, 1e-12) * DIM ** 0.5 * gamma

        def _safe_cumprod(t, axis):
            t = jnp.clip(t, EPS_CUMPROD, 1.0)
            return jnp.exp(jnp.cumsum(jnp.log(t), axis=axis))
        key = jax.random.key(seed)
        ks = jax.random.split(key, 8)
        b, n = (2, 512)
        x = jax.random.normal(ks[0], (b, n, DIM), dtype=jnp.float32)
        gamma = jnp.ones((DIM,), dtype=jnp.float32)
        w_qkv = jax.random.normal(ks[1], (DIM, 3 * DIM_INNER), dtype=jnp.float32) * 0.02
        b_qkv = jnp.zeros((3 * DIM_INNER,), dtype=jnp.float32)
        w_a = jax.random.normal(ks[2], (DIM, DIM_INNER), dtype=jnp.float32) * 0.02
        b_a = jnp.full((DIM_INNER,), 2.0, dtype=jnp.float32)
        w_out = jax.random.normal(ks[3], (DIM_INNER, DIM), dtype=jnp.float32) * 0.02
        b_out = jnp.zeros((DIM,), dtype=jnp.float32)
        return {'x': x, 'gamma': gamma, 'w_qkv': w_qkv, 'b_qkv': b_qkv, 'w_a': w_a, 'b_a': b_a, 'w_out': w_out, 'b_out': b_out}
    _L0_attn_all = _L0_attn_setup()
    _L0_attn_in = {k: v for k, v in _L0_attn_all.items() if k in ('gamma', 'w_qkv', 'b_qkv', 'w_a', 'b_a', 'w_out', 'b_out')}
    del _L0_attn_all

    def _L0_ffn_setup():
        import jax, jax.numpy as jnp
        import numpy as np
        B, S, D = (8, 1024, 128)
        H = 512
        O = 128
        E = 8
        TOP_K = 1
        key = jax.random.key(seed)
        ks = jax.random.split(key, 8)
        sc = 0.02
        return {'x': jax.random.normal(ks[0], (B, S, D), dtype=jnp.float32), 'Wr': jax.random.normal(ks[1], (D, E), dtype=jnp.float32) * sc, 'br': jnp.zeros((E,), dtype=jnp.float32), 'W1': jax.random.normal(ks[2], (E, D, H), dtype=jnp.float32) * sc, 'b1': jnp.zeros((E, H), dtype=jnp.float32), 'W2': jax.random.normal(ks[3], (E, H, O), dtype=jnp.float32) * sc, 'b2': jnp.zeros((E, O), dtype=jnp.float32)}
    _L0_ffn_all = _L0_ffn_setup()
    _L0_ffn_in = {k: v for k, v in _L0_ffn_all.items() if k in ('Wr', 'br', 'W1', 'b1', 'W2', 'b2')}
    del _L0_ffn_all
    return {'x': x, 'L0_tok_emb': _L0_tok_in['emb'], 'L0_tok_ln0_g': _L0_tok_in['ln0_g'], 'L0_tok_ln0_b': _L0_tok_in['ln0_b'], 'L0_tok_W1': _L0_tok_in['W1'], 'L0_tok_g1': _L0_tok_in['g1'], 'L0_tok_b1': _L0_tok_in['b1'], 'L0_tok_W2': _L0_tok_in['W2'], 'L0_tok_g2': _L0_tok_in['g2'], 'L0_tok_b2': _L0_tok_in['b2'], 'L0_attn_gamma': _L0_attn_in['gamma'], 'L0_attn_w_qkv': _L0_attn_in['w_qkv'], 'L0_attn_b_qkv': _L0_attn_in['b_qkv'], 'L0_attn_w_a': _L0_attn_in['w_a'], 'L0_attn_b_a': _L0_attn_in['b_a'], 'L0_attn_w_out': _L0_attn_in['w_out'], 'L0_attn_b_out': _L0_attn_in['b_out'], 'L0_ffn_Wr': _L0_ffn_in['Wr'], 'L0_ffn_br': _L0_ffn_in['br'], 'L0_ffn_W1': _L0_ffn_in['W1'], 'L0_ffn_b1': _L0_ffn_in['b1'], 'L0_ffn_W2': _L0_ffn_in['W2'], 'L0_ffn_b2': _L0_ffn_in['b2']}

def reference(x, L0_tok_emb, L0_tok_ln0_g, L0_tok_ln0_b, L0_tok_W1, L0_tok_g1, L0_tok_b1, L0_tok_W2, L0_tok_g2, L0_tok_b2, L0_attn_gamma, L0_attn_w_qkv, L0_attn_b_qkv, L0_attn_w_a, L0_attn_b_a, L0_attn_w_out, L0_attn_b_out, L0_ffn_Wr, L0_ffn_br, L0_ffn_W1, L0_ffn_b1, L0_ffn_W2, L0_ffn_b2):
    import jax
    import jax.numpy as jnp

    def _L0_tok_ref(tokens, emb, ln0_g, ln0_b, W1, g1, b1, W2, g2, b2):
        import jax, jax.numpy as jnp
        import numpy as np
        B, S, H, L, V, PAD = (32, 256, 128, 8, 33, 1)

        def layer_norm(x, g, b, eps):
            mu = jnp.mean(x, axis=-1, keepdims=True)
            var = jnp.mean(jnp.square(x - mu), axis=-1, keepdims=True)
            return (x - mu) * jax.lax.rsqrt(var + eps) * g + b

        def conv1d_same(x, w):
            return jax.lax.conv_general_dilated(x, w, window_strides=(1,), padding=[(1, 1)], dimension_numbers=('NWC', 'WIO', 'NWC'))
        dt = emb.dtype
        pad = tokens == PAD
        x = emb[tokens]
        s = x.shape[1]
        pos = jnp.arange(s - 1, -1, -1, dtype=dt)
        inv_freq = 1.0 / 10000.0 ** (jnp.arange(0.0, H, 2.0, dtype=dt) / H)
        sin_in = pos[:, None] * inv_freq[None, :]
        pe = jnp.concatenate([jnp.sin(sin_in), jnp.cos(sin_in)], axis=-1)
        x = x + pe[None]
        x = layer_norm(x, ln0_g, ln0_b, 1e-12)
        x = x * (1.0 - pad[..., None].astype(dt))
        for i in range(W1.shape[0]):
            r = x
            h = conv1d_same(x, W1[i])
            h = layer_norm(h, g1[i], b1[i], 1e-05)
            h = jax.nn.relu(h)
            h = conv1d_same(h, W2[i])
            h = layer_norm(h, g2[i], b2[i], 1e-05)
            x = h + r
        return x

    def _L0_attn_ref(x, gamma, w_qkv, b_qkv, w_a, b_a, w_out, b_out):
        import jax, jax.numpy as jnp
        import numpy as np
        DIM = 128
        HEADS = 8
        DIM_HEAD = 64
        DIM_INNER = HEADS * DIM_HEAD
        FRAC_GRAD = 0.5
        SCALE = DIM_HEAD ** (-0.5)
        EPS_CUMPROD = 1e-10
        EPS_INV = 1e-08

        def _rms_norm(x, gamma):
            nrm = jnp.linalg.norm(x, axis=-1, keepdims=True)
            return x / jnp.maximum(nrm, 1e-12) * DIM ** 0.5 * gamma

        def _safe_cumprod(t, axis):
            t = jnp.clip(t, EPS_CUMPROD, 1.0)
            return jnp.exp(jnp.cumsum(jnp.log(t), axis=axis))
        b, n, _ = x.shape
        x = _rms_norm(x, gamma)
        qkv = x @ w_qkv + b_qkv
        qkv = qkv.reshape(b, n, 3, HEADS, DIM_HEAD).transpose(2, 0, 3, 1, 4)
        q, k, v = (qkv[0], qkv[1], qkv[2])
        q = q * SCALE
        a = (x @ w_a + b_a).reshape(b, n, HEADS, DIM_HEAD).transpose(0, 2, 1, 3)
        a = a * FRAC_GRAD + jax.lax.stop_gradient(a) * (1.0 - FRAC_GRAD)
        a = jax.nn.sigmoid(a)
        a_cum = _safe_cumprod(a, axis=-2)
        a_cum_inv = 1.0 / jnp.maximum(a_cum, EPS_INV)
        q = q * a_cum
        k = k * a_cum_inv
        sim = jnp.einsum('bhid,bhjd->bhij', q, k)
        causal_mask = jnp.triu(jnp.ones((n, n), dtype=bool), k=1)
        attn = jnp.where(causal_mask, 0.0, sim)
        out = jnp.einsum('bhij,bhjd->bhid', attn, v)
        out = out.transpose(0, 2, 1, 3).reshape(b, n, DIM_INNER)
        return out @ w_out + b_out

    def _L0_ffn_ref(x, Wr, br, W1, b1, W2, b2):
        import jax, jax.numpy as jnp
        import numpy as np
        B, S, D = (8, 1024, 128)
        H = 512
        O = 128
        E = 8
        TOP_K = 1
        b, s, d = x.shape
        xf = x.reshape(-1, d)
        router_logits = xf @ Wr + br
        topk_logits, topk_idx = jax.lax.top_k(router_logits, TOP_K)
        topk_gates = jax.nn.softmax(topk_logits, axis=1)
        out = jnp.zeros((xf.shape[0], O), dtype=x.dtype)
        for k in range(TOP_K):
            idx_k = topk_idx[:, k]
            gate_k = topk_gates[:, k:k + 1]
            for e in range(E):
                h = jax.nn.relu(xf @ W1[e] + b1[e])
                oe = h @ W2[e] + b2[e]
                mask = (idx_k == e)[:, None]
                out = out + jnp.where(mask, gate_k * oe, 0.0)
        return out.reshape(b, s, O)
    h = _L0_tok_ref(x, L0_tok_emb, L0_tok_ln0_g, L0_tok_ln0_b, L0_tok_W1, L0_tok_g1, L0_tok_b1, L0_tok_W2, L0_tok_g2, L0_tok_b2)
    h = h + _L0_attn_ref(_layernorm(h, axis=-1), L0_attn_gamma, L0_attn_w_qkv, L0_attn_b_qkv, L0_attn_w_a, L0_attn_b_a, L0_attn_w_out, L0_attn_b_out)
    h = h + _L0_ffn_ref(_layernorm(h, axis=-1), L0_ffn_Wr, L0_ffn_br, L0_ffn_W1, L0_ffn_b1, L0_ffn_W2, L0_ffn_b2)
    return h

_drawn_inputs = setup_inputs


def setup_inputs(seed=0):
    import zlib

    import numpy as np

    out = dict(_drawn_inputs(seed))
    spreads = {'L0_tok_ln0_g': (1.0, 0.2),
     'L0_tok_ln0_b': (0.0, 0.1),
     'L0_tok_g1': (1.0, 0.2),
     'L0_tok_b1': (0.0, 0.1),
     'L0_tok_g2': (1.0, 0.2),
     'L0_tok_b2': (0.0, 0.1),
     'L0_attn_gamma': (1.0, 0.6),
     'L0_attn_b_qkv': (0.0, 0.658),
     'L0_attn_b_a': (2.0, 0.6),
     'L0_attn_b_out': (0.0, 0.8),
     'L0_ffn_br': (0.0, 0.8),
     'L0_ffn_b1': (0.0, 2.0),
     'L0_ffn_b2': (0.0, 0.8)}
    factors = {'L0_attn_w_qkv': 3.523,
     'L0_attn_w_a': 8.0,
     'L0_attn_w_out': 3.213,
     'L0_ffn_W1': 21.792,
     'L0_ffn_Wr': 8.0,
     'L0_ffn_W2': 8.0}
    for name, (base, spread) in spreads.items():
        noise = np.random.default_rng([zlib.crc32(name.encode()), seed]).standard_normal(out[name].shape)
        drawn = base * np.exp(spread * noise) if base else spread * noise
        out[name] = jnp.asarray(drawn.astype(out[name].dtype))
    for name, factor in factors.items():
        out[name] = (out[name] * factor).astype(out[name].dtype)
    return out
```

```python
from contextlib import ExitStack

import numpy as np

import concourse.bass as bass
from concourse import mybir

F32 = mybir.dt.float32
I32 = mybir.dt.int32
U32 = mybir.dt.uint32
ALU = mybir.AluOpType
ACT = mybir.ActivationFunctionType
AX = mybir.AxisListType

P = 128
B, S, C = 8, 512, 128
NB = S // P
LAYERS, VOCAB, PAD = 8, 33, 1
HEADS, DH = 8, 64
DI = HEADS * DH
PAIRS = HEADS // 2
EXPERTS, HID = 8, 512
TB = B * NB
SLOT_BLOCKS = 2 * (((B * S + EXPERTS * (P - 1)) // P + 1) // 2)

EPS_EMB, EPS_CONV, EPS_LN = 1e-12, 1e-5, 1e-5
VAR_FLOOR = 1e-24 * EPS_LN / C
DECAY_FLOOR, INV_FLOOR = 1e-10, 1e-8
Q_SCALE = DH ** -0.5

R_G2, R_B2, R_G1, R_B1 = 0, LAYERS + 1, 2 * (LAYERS + 1), 3 * LAYERS + 2
R_GAMMA = R_B1 + LAYERS
R_BOUT, R_BQ = R_GAMMA + 1, R_GAMMA + 2
R_BK, R_BA = R_BQ + PAIRS, R_BQ + 2 * PAIRS
ROWS = R_BA + PAIRS

U_CONV = B
U_LN1 = U_CONV + 2 * B * LAYERS
U_LN2 = U_LN1 + B
UNITS = U_LN2 + B


class Unit:

    def __init__(self, kind, b, n, n0, layer=0):
        self.kind, self.b, self.n, self.n0, self.layer = kind, b, n, n0, layer

    @property
    def slot(self):
        return self.n0 % 4

    @property
    def side(self):
        return self.n0 % 2

    @property
    def update(self):
        return self.b if self.kind == "embed" else B + B * self.layer + self.b


def conv_unit(which, layer, b):
    n = U_CONV + 2 * B * layer + (B if which == "conv2" else 0) + b
    return Unit(which, b, n, (B if which == "conv2" else 0) + b, layer)


def head_units():
    return [Unit("embed", b, b, b) for b in range(B)] + [conv_unit("conv1", 0, b) for b in (0, 1)]


def layer_units(l):
    return ([conv_unit("conv1", l, b) for b in range(2, B)] + [conv_unit("conv2", l, b) for b in range(B)]
            + [conv_unit("conv1", l + 1, b) for b in (0, 1)])


def tail_units():
    return layer_units(LAYERS - 1)[:-2] + [Unit("ln1", b, U_LN1 + b, b) for b in range(B)]


def ln2_units():
    return [Unit("ln2", b, U_LN2 + b, b) for b in range(B)]


def walk(eng, step):
    def run(units, before):
        chain = before + units
        for i in range(2, len(chain)):
            step(chain[i], chain[i - 1], chain[i - 2])

    run(head_units(), [None, None])
    with eng.Fori(0, LAYERS - 1) as l:
        run(layer_units(l), [conv_unit("conv1", l, 0), conv_unit("conv1", l, 1)])
    run(tail_units() + [None, None], [conv_unit("conv1", LAYERS - 1, 0), conv_unit("conv1", LAYERS - 1, 1)])


def walk_ln2(step):
    chain = [None, None] + ln2_units() + [None, None]
    for i in range(2, len(chain)):
        step(chain[i], chain[i - 1], chain[i - 2])


class Block:

    def __init__(self, i, side, half):
        self.i, self.side, self.half = i, side, half


def walk_blocks(eng, step):
    def static(i):
        return Block(i, i % 2, i // 2) if 0 <= i < SLOT_BLOCKS else None

    for i in range(-1, 3):
        step(static(i), static(i - 1), static(i + 1))
    with eng.Fori(1, SLOT_BLOCKS // 2 - 1) as r:
        for k in (1, 2):
            step(*(Block(2 * r + k + d, (k + d) % 2, r + (k + d) // 2) for d in (0, -1, 1)))
    for i in range(SLOT_BLOCKS - 1, SLOT_BLOCKS + 1):
        step(static(i), static(i - 1), static(i + 1))


def tower(nc, x, emb, ln0_g, ln0_b, W1, g1, b1, W2, g2, b2, gamma, w_qkv, b_qkv, w_a, b_a, w_out, b_out,
          Wr, br, E1, eb1, E2, eb2, pe, ident_in, causal_in, before_in, ramps_in, out):
    with ExitStack() as ctx:
        def sb(name, shape, dt=F32):
            return ctx.enter_context(nc.sbuf_tensor(name, shape, dt))

        def sem(name):
            return ctx.enter_context(nc.semaphore(name))

        ident = sb("ident", [P, P])
        causal = sb("causal", [P, P])
        before = sb("before", [P, P])
        ones = sb("ones", [P, S])
        ramps = sb("ramps", [P, EXPERTS + TB + SLOT_BLOCKS])
        table = sb("table", [ROWS, C])
        cols = sb("cols", [P, ROWS])
        nba = sb("nba", [P, PAIRS])
        bqs = sb("bqs", [P, PAIRS])
        eps_emb = sb("eps_emb", [P, 1])
        eps_conv = sb("eps_conv", [P, 1])
        zero_col = sb("zero_col", [P, 1])
        iota_p = sb("iota_p", [P, 1])
        emb_sb = sb("emb_sb", [VOCAB, C])
        pe_sb = sb("pe_sb", [P, NB, C])
        tok = sb("tok", [P, S * 2], I32)
        onehot = sb("onehot", [VOCAB, 2, S])
        notpad = sb("notpad", [P, 4, S])
        w_conv = sb("w_conv", [P, 2, LAYERS * 3, C])
        wqkv_sb = sb("wqkv_sb", [P, 3 * DI])
        wa_sb = sb("wa_sb", [P, DI])
        wout_sb = sb("wout_sb", [P, PAIRS, C])
        bv_rep = sb("bv_rep", [P, DI])
        wr_sb = sb("wr_sb", [P, EXPERTS])
        br_rep = sb("br_rep", [P, EXPERTS])
        e1_sb = sb("e1_sb", [P, EXPERTS * HID])
        e2_sb = sb("e2_sb", [P, EXPERTS * HID // P * C])
        eb1_rep = sb("eb1_rep", [P, EXPERTS * HID])
        eb2_rep = sb("eb2_rep", [P, EXPERTS * C])

        res = sb("res", [P, B, S + 2])
        mid = sb("mid", [P, B, S + 2])
        bns = sb("bns", [P, 4, NB, 6])
        mv = sb("mv", [P, 4, NB, 2])
        std = sb("std", [P, 4, NB])
        rstd = sb("rstd", [P, 4, NB])
        xe = sb("xe", [P, 2, NB, C])
        xn = sb("xn", [P, 2, NB, C])
        delta = sb("delta", [P, 2, S])

        xs = sb("xs", [P, S])
        arena = sb("arena", [P, 8, S])
        expa, soft, cum, cumc, decay, inv_decay = (arena[:, i, :] for i in range(6))
        qd = arena[:, 6:8, :]
        xf = arena[:, :, :].rearrange("p a (n c) -> p (a n) c", c=C)
        kd = sb("kd", [P, 2, S])
        kn = sb("kn", [P, NB - 1, P])
        vv = notpad
        probs = sb("probs", [P, 2, 2, P])
        state = sb("state", [P, 2, P])
        att = sb("att", [P, PAIRS, S])

        htok = w_conv[:, :, :, :].rearrange("p w k c -> p (w k) c")[:, 0:TB, :]
        small = sb("small", [P, 12, EXPERTS * TB])
        slot_u = sb("slot_u", [P, TB], U32)
        blk_e = sb("blk_e", [P, SLOT_BLOCKS], I32)
        xb = sb("xb", [P, 2, C])
        xbt = sb("xbt", [P, 2, P])
        hb, hbt = att[:, 0:2, :], att[:, 2:4, :]
        yb = sb("yb", [P, 2, C])

        xs_dram = nc.dram_tensor("xs_dram", [SLOT_BLOCKS * P, C], F32, kind="Internal").ap()
        ys_dram = nc.dram_tensor("ys_dram", [SLOT_BLOCKS * P, C], F32, kind="Internal").ap()

        psum = ctx.enter_context(nc.psum_tensor("psum", [P, 8, 512], F32))
        bank = [psum[:, i, :] for i in range(8)]
        Y = bank[0:4]
        T = bank[4:6]
        ps_ak, ps_q, ps_kso, ps_o = bank[0:4]
        ps_s = bank[4:8]

        top = small[:, 1, 0:TB]
        gate_arg, gate_exp = small[:, 1, 3 * TB:4 * TB], small[:, 1, 4 * TB:5 * TB]
        gate_inv, gate = small[:, 1, 5 * TB:6 * TB], small[:, 1, 6 * TB:7 * TB]
        chosen = small[:, 4, :]

        s_tok = [sem("tokens_loaded_0"), sem("tokens_loaded_1")]
        s_ld0 = sem("first_constants_loaded")
        s_ldw = sem("conv_weights_loaded")
        s_ldr = sem("rest_loaded")
        s_const = sem("constants_made")
        s_colps = sem("columns_turned")
        s_col = sem("columns_ready")
        s_scaled = sem("q_weights_scaled")
        s_hot = sem("onehot_ready")
        s_y = sem("y_ready")
        s_xe = sem("xe_ready")
        s_bn = sem("bn_stats_done")
        s_ag = sem("aggregated")
        s_var = sem("var_ready")
        s_std = sem("std_ready")
        s_rstd = sem("rstd_ready")
        s_xn = sem("xn_ready")
        s_t = sem("t_ready")
        s_aff = sem("affine_done")
        s_res = sem("residual_updated")
        s_ht = sem("htok_copied")

        s_xs = sem("row_staged")
        s_aps, s_qps, s_kps = sem("a_projected"), sem("q_projected"), sem("k_projected")
        s_e, s_em, s_sp, s_scan = sem("exp_done"), sem("exp_clipped"), sem("softplus_done"), sem("scan_done")
        s_cc, s_dec, s_inv = sem("cum_clipped"), sem("decay_ready"), sem("inv_decay_ready")
        s_q, s_k = sem("q_ready"), sem("k_ready")
        s_vps, s_v = sem("v_projected"), sem("v_ready")
        s_knps, s_kn = sem("k_turned"), sem("kn_ready")
        s_sps, s_p = sem("scores_ready"), sem("probs_ready")
        s_stps, s_st = sem("state_product_ready"), sem("state_ready")
        s_pv = sem("chunk_output_ready")
        s_att = sem("att_ready")
        s_ops, s_h = sem("out_projected"), sem("attention_added")

        s_lg = sem("logits_ready")
        s_d = sem("dispatch_step")
        s_gexp = sem("gate_exp_done")
        s_rank = sem("ranks_ready")
        s_zero = sem("slots_zeroed")
        s_scat = sem("tokens_scattered")
        s_xb = [sem("block_loaded_0"), sem("block_loaded_1")]
        s_xbps, s_xbt = sem("block_turned"), sem("xbt_ready")
        s_hps, s_hb = sem("hidden_ready"), sem("hidden_biased")
        s_htps, s_hbt = sem("hidden_turned"), sem("hbt_ready")
        s_yps, s_yb = sem("expert_out_ready"), sem("yb_ready")
        s_yst = [sem("block_stored_0"), sem("block_stored_1")]
        s_gat = [sem(f"outputs_gathered_{b}") for b in range(B)]
        s_fin = sem("rows_finished")
        s_out = sem("outputs_stored")

        block = ctx.enter_context(nc.Block())

        def wait(eng, s, value):
            if not isinstance(value, int) or value > 0:
                eng.wait_ge(s, value)

        CONSTS = 11
        FIRST_LOADS, REST_LOADS = 13, 13
        CHOSEN_STEP, GATE_STEP, SLOT_STEP, DISPATCH_STEPS = 7, 8, 24, 27

        def block_expert(eng, blk):
            return eng.value_load(blk_e[0:1, bass.ds(blk.i, 1)], min_val=0, max_val=EXPERTS - 1)

        @block.sync
        def _(sp):
            def load_tokens(b):
                if b >= 2:
                    sp.wait_ge(s_hot, b - 1)
                sp.dma_start(tok[:, (b % 2) * S:(b % 2 + 1) * S], x[b].partition_broadcast(P)).then_inc(s_tok[b % 2], 16)

            load_tokens(0)
            load_tokens(1)
            sp.dma_start(ident[:, :], ident_in).then_inc(s_ld0, 16)
            for r, src in ((R_G2, ln0_g), (R_B2, ln0_b), (R_GAMMA, gamma), (R_BOUT, b_out)):
                sp.dma_start(table[r:r + 1, :], src.rearrange("(a c) -> a c", a=1)).then_inc(s_ld0, 16)
            for r, src in ((R_G2 + 1, g2), (R_B2 + 1, b2), (R_G1, g1), (R_B1, b1)):
                sp.dma_start(table[r:r + LAYERS, :], src).then_inc(s_ld0, 16)
            sp.dma_start(table[R_BQ:R_BQ + 2 * PAIRS, :],
                         b_qkv[0:2 * DI].rearrange("(a c) -> a c", c=C)).then_inc(s_ld0, 16)
            sp.dma_start(table[R_BA:R_BA + PAIRS, :], b_a.rearrange("(a c) -> a c", c=C)).then_inc(s_ld0, 16)
            sp.dma_start(emb_sb[:, :], emb).then_inc(s_ld0, 16)
            sp.dma_start(pe_sb[:, :, :], pe.rearrange("(n p) c -> p n c", p=P)).then_inc(s_ld0, 16)
            for i, w in enumerate((W1, W2)):
                sp.dma_start(w_conv[:, i, :, :], w.rearrange("l k i o -> i (l k) o")).then_inc(s_ldw, 16)
            sp.dma_start(causal[:, :], causal_in).then_inc(s_ldr, 16)
            sp.dma_start(before[:, :], before_in).then_inc(s_ldr, 16)
            sp.dma_start(ramps[:, :], ramps_in.partition_broadcast(P)).then_inc(s_ldr, 16)
            sp.dma_start(wqkv_sb[:, :], w_qkv).then_inc(s_ldr, 16)
            sp.dma_start(wa_sb[:, :], w_a).then_inc(s_ldr, 16)
            sp.dma_start(wout_sb[:, :, :], w_out.rearrange("(h p) c -> p h c", p=P)).then_inc(s_ldr, 16)
            sp.dma_start(bv_rep[:, :], b_qkv[2 * DI:3 * DI].partition_broadcast(P)).then_inc(s_ldr, 16)
            sp.dma_start(wr_sb[:, :], Wr).then_inc(s_ldr, 16)
            sp.dma_start(br_rep[:, :], br.partition_broadcast(P)).then_inc(s_ldr, 16)
            sp.dma_start(e1_sb[:, :].rearrange("p (e h) -> p e h", e=EXPERTS),
                         E1.rearrange("e c h -> c e h")).then_inc(s_ldr, 16)
            sp.dma_start(e2_sb[:, :].rearrange("p (a c) -> p a c", c=C),
                         E2.rearrange("e (n p) c -> p (e n) c", p=P)).then_inc(s_ldr, 16)
            sp.dma_start(eb1_rep[:, :], eb1.rearrange("e h -> (e h)").partition_broadcast(P)).then_inc(s_ldr, 16)
            sp.dma_start(eb2_rep[:, :], eb2.rearrange("e c -> (e c)").partition_broadcast(P)).then_inc(s_ldr, 16)
            sp.wait_ge(s_const, 1)
            zeros = small[:, :, :].rearrange("p t c -> p (t c)")[:, 0:SLOT_BLOCKS * C // 2]
            for half in range(2):
                rows = xs_dram[half * SLOT_BLOCKS * P // 2:(half + 1) * SLOT_BLOCKS * P // 2, :]
                sp.dma_start(rows.rearrange("(p r) c -> p (r c)", p=P), zeros).then_inc(s_zero, 16)

            for b in range(2, B):
                load_tokens(b)
            sp.wait_ge(s_scat, 16 * TB)

            def load_block(cur, _, nxt):
                if nxt is None:
                    return
                wait(sp, s_xbps, nxt.i - 1)
                sp.dma_start(xb[:, nxt.side, :], xs_dram[bass.ds(nxt.i * P, P), :]).then_inc(s_xb[nxt.side], 16)

            walk_blocks(sp, load_block)

            for b in range(B):
                sp.wait_ge(s_fin, b + 1)
                sp.dma_start(out[b].rearrange("(n p) c -> p n c", p=P),
                             htok[:, b * NB:(b + 1) * NB, :]).then_inc(s_out, 16)
            sp.wait_ge(s_out, 16 * B)

        @block.gpsimd
        def _(pool):
            pool.memset(small[:, :, :], 0.0).then_inc(s_const, 1)
            pool.memset(eps_emb[:, :], EPS_EMB).then_inc(s_const, 1)
            pool.memset(eps_conv[:, :], EPS_CONV).then_inc(s_const, 1)
            pool.memset(zero_col[:, :], 0.0).then_inc(s_const, 1)
            pool.memset(ones[:, :], 1.0).then_inc(s_const, 1)
            pool.memset(state[:, :, :], 0.0).then_inc(s_const, 1)
            for buf in (res, mid):
                for edge in (0, S + 1):
                    pool.memset(buf[:, :, edge:edge + 1], 0.0).then_inc(s_const, 1)
            pool.iota(iota_p[:, :], [[0, 1]], base=0, channel_multiplier=1,
                      allow_small_or_imprecise_dtypes=True).then_inc(s_const, 1)
            def step(u, _, lag):
                if lag is None or lag.kind not in ("embed", "conv2"):
                    return
                row = res[:, lag.b, 1:S + 1]
                pool.wait_ge(s_aff, lag.n + 1)
                if lag.kind == "embed":
                    pool.wait_ge(s_hot, lag.b + 1)
                    pool.tensor_tensor(row, delta[:, lag.side, :], notpad[:, lag.b % 4, :],
                                       ALU.mult).then_inc(s_res, 1)
                else:
                    pool.tensor_tensor(row, row, delta[:, lag.side, :], ALU.add).then_inc(s_res, 1)

            walk(pool, step)

            pool.wait_ge(s_ldr, 16 * REST_LOADS)
            pool.wait_ge(s_col, 1)
            pool.tensor_scalar(wqkv_sb[:, 0:DI], wqkv_sb[:, 0:DI], Q_SCALE, None, ALU.mult).then_inc(s_scaled, 1)
            pool.tensor_scalar(bqs[:, :], cols[:, R_BQ:R_BQ + PAIRS], Q_SCALE, None, ALU.mult).then_inc(s_scaled, 1)
            pool.tensor_scalar(nba[:, :], cols[:, R_BA:R_BA + PAIRS], -1.0, None, ALU.mult).then_inc(s_scaled, 1)
            for b in range(B):
                pool.wait_ge(s_aff, U_LN1 + b + 1)
                if b:
                    pool.wait_ge(s_kps, PAIRS * b)
                pool.tensor_copy(xs[:, :], mid[:, b, 1:S + 1]).then_inc(s_xs, 1)

            pool.wait_ge(s_d, SLOT_STEP)
            pool.wait_ge(s_xn, UNITS)
            pool.wait_ge(s_zero, 32)
            for t in range(TB):
                pool.indirect_dma_start(out=xs_dram, out_offset=bass.IndirectOffsetOnAxis(ap=slot_u[:, t:t + 1], axis=0),
                                        in_=xf[:, t, :], in_offset=None).then_inc(s_scat, 16)
            pool.wait_ge(s_scat, 16 * TB)
            for side in range(2):
                pool.wait_ge(s_yst[side], 16 * SLOT_BLOCKS // 2)
            for t in range(TB):
                pool.indirect_dma_start(out=xf[:, t, :], out_offset=None, in_=ys_dram,
                                        in_offset=bass.IndirectOffsetOnAxis(ap=slot_u[:, t:t + 1], axis=0)
                                        ).then_inc(s_gat[t // NB], 16)

        @block.scalar
        def _(act):
            act.wait_ge(s_const, CONSTS)

            def root(u):
                eps = {"embed": eps_emb, "ln1": zero_col}.get(u.kind, eps_conv)
                act.activation(std[:, u.slot, :], mv[:, u.slot, :, 1], ACT.Sqrt, bias=eps[:, 0:1]).then_inc(s_std, 1)

            def affine(u):
                src = T[u.side][:, :]
                row = mid[:, u.b, 1:S + 1]
                if u.kind == "conv1":
                    act.activation(row, src, ACT.Relu, bias=cols[:, bass.ds(R_B1 + u.layer, 1)],
                                   scale=cols[:, bass.ds(R_G1 + u.layer, 1)]).then_inc(s_aff, 1)
                elif u.kind in ("embed", "conv2"):
                    k = 0 if u.kind == "embed" else u.layer + 1
                    act.activation(delta[:, u.side, :], src, ACT.Identity, bias=cols[:, bass.ds(R_B2 + k, 1)],
                                   scale=cols[:, bass.ds(R_G2 + k, 1)]).then_inc(s_aff, 1)
                elif u.kind == "ln1":
                    act.activation(row, src, ACT.Copy, scale=cols[:, R_GAMMA:R_GAMMA + 1]).then_inc(s_aff, 1)
                else:
                    act.activation(row, src, ACT.Copy).then_inc(s_aff, 1)

            def waits(u, lag):
                if u is not None:
                    act.wait_ge(s_var, u.n + 1)
                if lag is not None:
                    act.wait_ge(s_t, lag.n + 1)
                    if lag.kind in ("embed", "conv2"):
                        wait(act, s_res, lag.update - 1)

            def step(u, _, lag):
                waits(u, lag)
                if u is not None:
                    root(u)
                if lag is not None:
                    affine(lag)

            act.wait_ge(s_col, 1)
            walk(act, step)

            def decay_chain(m, pair, part):
                if part == 0:
                    act.wait_ge(s_aps, m + 1)
                    wait(act, s_sp, m)
                    act.activation(expa, ps_ak, ACT.Exp, bias=nba[:, pair:pair + 1],
                                   scale=-1.0).then_inc(s_e, 1)
                    act.wait_ge(s_em, m + 1)
                    wait(act, s_scan, m)
                    act.activation(soft, expa, ACT.Ln, bias=ones[:, 0:1]).then_inc(s_sp, 1)
                else:
                    act.wait_ge(s_scan, m + 1)
                    wait(act, s_q, m)
                    act.activation(decay, cum, ACT.Exp, scale=-1.0).then_inc(s_dec, 1)
                    act.wait_ge(s_cc, m + 1)
                    wait(act, s_k, m)
                    act.activation(inv_decay, cumc, ACT.Exp).then_inc(s_inv, 1)

            def attend(m, pair, last):
                act.wait_ge(s_knps, m + 1)
                act.activation(kn[:, :, :], ps_kso[:, 0:(NB - 1) * P].rearrange("p (n c) -> p n c", c=P),
                               ACT.Copy).then_inc(s_kn, 1)
                if not last:
                    decay_chain(m + 1, (pair + 1) % PAIRS, 0)
                    decay_chain(m + 1, (pair + 1) % PAIRS, 1)
                act.wait_ge(s_pv, NB * (m + 1))
                act.activation(att[:, pair, :], ps_o[:, :], ACT.Copy).then_inc(s_att, 1)

            act.wait_ge(s_scaled, 3)
            decay_chain(0, 0, 0)
            decay_chain(0, 0, 1)
            with act.Fori(0, B - 1) as b:
                for pair in range(PAIRS):
                    attend(b * PAIRS + pair, pair, False)
            for pair in range(PAIRS):
                attend((B - 1) * PAIRS + pair, pair, pair == PAIRS - 1)

            def step2(u, _, lag):
                if u is not None:
                    act.wait_ge(s_y, u.n + 1)
                    act.activation(htok[:, u.b * NB:(u.b + 1) * NB, :],
                                   Y[u.slot].rearrange("p (n c) -> p n c", c=C), ACT.Copy).then_inc(s_ht, 1)
                waits(u, lag)
                if u is not None:
                    root(u)
                if lag is not None:
                    affine(lag)

            walk_ln2(step2)

            act.wait_ge(s_d, GATE_STEP)
            act.activation(gate_exp, gate_arg, ACT.Exp).then_inc(s_gexp, 1)

            def block_step(cur, prev, nxt):
                if nxt is not None:
                    act.wait_ge(s_xbps, nxt.i + 1)
                    wait(act, s_hps, nxt.i - 1)
                    act.activation(xbt[:, nxt.side, :], bank[nxt.side][:, 0:P], ACT.Copy).then_inc(s_xbt, 1)
                if prev is not None:
                    act.wait_ge(s_htps, prev.i + 1)
                    wait(act, s_yps, prev.i - 1)
                    act.activation(hbt[:, prev.side, :], bank[4 + prev.side], ACT.Relu).then_inc(s_hbt, 1)
                    act.wait_ge(s_yb, prev.i + 1)
                    act.dma_start(ys_dram[bass.ds(prev.i * P, P), :],
                                  yb[:, prev.side, :]).then_inc(s_yst[prev.side], 16)

            walk_blocks(act, block_step)
            for side in range(2):
                act.wait_ge(s_yst[side], 16 * SLOT_BLOCKS // 2)

        @block.tensor
        def _(pe):
            pe.wait_ge(s_ld0, 16 * FIRST_LOADS)
            pe.transpose(T[1][:, 0:ROWS], table[:, :], ident[0:ROWS, 0:ROWS]).then_inc(s_colps, 1)
            pe.wait_ge(s_const, CONSTS)
            pe.wait_ge(s_col, 1)

            def produce(u):
                y = Y[u.slot]
                wait(pe, s_xn, u.n - 3)
                if u.kind == "ln2":
                    wait(pe, s_ht, u.b - 3)
                if u.kind == "embed":
                    pe.wait_ge(s_hot, u.b + 1)
                    for j in range(NB):
                        mm = pe.matmul(y[:, j * C:(j + 1) * C], onehot[:, u.b % 2, j * P:(j + 1) * P],
                                       emb_sb[:, :], start=True, stop=True)
                elif u.kind in ("conv1", "conv2"):
                    if u.kind == "conv1":
                        pe.wait_ge(s_res, B * u.layer + u.b + 1)
                    else:
                        pe.wait_ge(s_aff, u.n - B + 1)
                    src = res if u.kind == "conv1" else mid
                    which = 0 if u.kind == "conv1" else 1
                    for j in range(NB):
                        for k in range(3):
                            mm = pe.matmul(y[:, j * C:(j + 1) * C], src[:, u.b, j * P + k:j * P + k + P],
                                           w_conv[:, which, bass.ds(u.layer * 3 + k, 1), :],
                                           start=(k == 0), stop=(k == 2))
                else:
                    if u.kind == "ln1":
                        pe.wait_ge(s_res, B * LAYERS + u.b + 1)
                    else:
                        pe.wait_ge(s_h, u.b + 1)
                    for j in range(NB):
                        mm = pe.transpose(y[:, j * C:(j + 1) * C], res[:, u.b, 1 + j * P:1 + (j + 1) * P],
                                          ident[:, :])
                mm.then_inc(s_y, 1)

            def turn(u):
                pe.wait_ge(s_xn, u.n + 1)
                wait(pe, s_aff, u.n - 1)
                for j in range(NB):
                    src = xf[:, u.b * NB + j, :] if u.kind == "ln2" else xn[:, u.side, j, :]
                    mm = pe.transpose(T[u.side][:, j * P:(j + 1) * P], src, ident[:, :])
                mm.then_inc(s_t, 1)

            def step(u, _, lag):
                if u is not None:
                    if u.kind == "conv1" and isinstance(u.n, int):
                        pe.wait_ge(s_ldw, 32)
                    produce(u)
                if lag is not None:
                    turn(lag)

            walk(pe, step)

            pe.wait_ge(s_ldr, 16 * REST_LOADS)
            pe.wait_ge(s_scaled, 3)
            pe.wait_ge(s_aff, U_LN2)
            pe.wait_ge(s_xn, U_LN2)

            def project_v(b):
                pe.wait_ge(s_xs, b + 1)
                for j in range(NB):
                    pe.matmul(ps_s[j], xs[:, j * P:(j + 1) * P], wqkv_sb[:, 2 * DI:3 * DI],
                              start=True, stop=True).then_inc(s_vps, 1)

            def project_aq(m, b, pair):
                f = slice(pair * P, (pair + 1) * P)
                pe.wait_ge(s_xs, b + 1)
                wait(pe, s_k, m)
                pe.matmul(ps_ak, wa_sb[:, f], xs[:, :], start=True, stop=True).then_inc(s_aps, 1)
                wait(pe, s_q, m)
                pe.matmul(ps_q, wqkv_sb[:, f], xs[:, :], start=True, stop=True).then_inc(s_qps, 1)

            def project_k(m, pair):
                pe.wait_ge(s_e, m + 1)
                pe.matmul(ps_ak, wqkv_sb[:, DI + pair * P:DI + (pair + 1) * P], xs[:, :],
                          start=True, stop=True).then_inc(s_kps, 1)

            def attend(m, b, pair, last):
                side = pair % 2

                def chunk(c):
                    return slice(c * P, (c + 1) * P)

                def scores(c):
                    if c >= 2:
                        pe.wait_ge(s_p, NB * m + c - 1)
                    for h in range(2):
                        rows = slice(h * DH, (h + 1) * DH)
                        mm = pe.matmul(ps_s[c % 2 * 2 + h][:, 0:P], kd[rows, side, chunk(c)],
                                       qd[rows, side, chunk(c)], start=True, stop=True)
                    mm.then_inc(s_sps, 1)

                def state_product(c):
                    if c == 0:
                        pe.wait_ge(s_kn, m + 1)
                    pe.matmul(ps_kso[:, 3 * P:4 * P], kn[:, c, :], vv[:, c, pair * P:(pair + 1) * P],
                              start=True, stop=True).then_inc(s_stps, 1)

                def from_state(c):
                    pe.wait_ge(s_st, (NB - 1) * m + c)
                    pe.matmul(ps_o[:, chunk(c)], state[:, (c - 1) % 2, :], qd[:, side, chunk(c)],
                              start=True, stop=False, skip_group_check=True)

                def from_chunk(c):
                    pe.wait_ge(s_p, NB * m + c + 1)
                    for h in range(2):
                        v = vv[:, c, pair * P + h * DH:pair * P + (h + 1) * DH]
                        mm = pe.matmul(ps_o[h * DH:(h + 1) * DH, chunk(c)], v, probs[:, c % 2, h, :],
                                       start=(c == 0), stop=True, skip_group_check=True)
                    mm.then_inc(s_pv, 1)

                pe.wait_ge(s_k, m + 1)
                for c in range(NB - 1):
                    mm = pe.transpose(ps_kso[:, chunk(c)], kd[:, side, chunk(c)], ident[:, :])
                mm.then_inc(s_knps, 1)
                pe.wait_ge(s_q, m + 1)
                if pair == 0:
                    pe.wait_ge(s_v, NB * (b + 1))
                scores(0)
                scores(1)
                state_product(0)
                if pair:
                    pe.wait_ge(s_att, m)
                from_chunk(0)
                if not (last and pair == PAIRS - 1):
                    project_k(m + 1, (pair + 1) % PAIRS)
                scores(2)
                from_state(1)
                state_product(1)
                from_chunk(1)
                scores(3)
                from_state(2)
                state_product(2)
                from_chunk(2)
                from_state(3)
                from_chunk(3)

            def project_out(b):
                pe.wait_ge(s_att, PAIRS * (b + 1))
                for pair in range(PAIRS):
                    mm = pe.matmul(ps_kso, wout_sb[:, pair, :], att[:, pair, :],
                                   start=(pair == 0), stop=(pair == PAIRS - 1))
                mm.then_inc(s_ops, 1)

            project_v(0)
            project_aq(0, 0, 0)
            project_k(0, 0)
            project_aq(1, 0, 1)

            def row(b, last):
                for pair in range(PAIRS):
                    m = PAIRS * b + pair
                    attend(m, b, pair, last)
                    if pair == PAIRS - 1:
                        if not last:
                            project_v(b + 1)
                        project_out(b)
                    if pair < 2:
                        project_aq(m + 2, b, pair + 2)
                    elif not last:
                        project_aq(m + 2, b + 1, pair - 2)
                    if pair == PAIRS - 1:
                        pe.wait_ge(s_h, b + 1)

            with pe.Fori(0, B - 1) as b:
                row(b, False)
            row(B - 1, True)

            walk_ln2(step)

            pe.wait_ge(s_aff, UNITS)
            for t in range(TB):
                b, j = divmod(t, NB)
                mm = pe.matmul(bank[6][:, t * EXPERTS:(t + 1) * EXPERTS], mid[:, b, 1 + j * P:1 + (j + 1) * P],
                               wr_sb[:, :], start=True, stop=True)
            mm.then_inc(s_lg, 1)
            pe.wait_ge(s_ht, B)
            pe.wait_ge(s_d, CHOSEN_STEP)
            pe.matmul(bank[0][:, 0:EXPERTS * TB], before[:, :], chosen, start=True, stop=True)
            pe.matmul(bank[1][:, 0:EXPERTS * TB], ones[:, 0:P], chosen, start=True, stop=True).then_inc(s_rank, 1)
            pe.wait_ge(s_d, DISPATCH_STEPS)

            def turn_x(blk):
                pe.wait_ge(s_xb[blk.side], 16 * (blk.half + 1))
                wait(pe, s_xbt, blk.i - 1)
                pe.transpose(bank[blk.side][:, 0:P], xb[:, blk.side, :], ident[:, :]).then_inc(s_xbps, 1)

            def block_step(cur, prev, nxt):
                if nxt is not None:
                    turn_x(nxt)
                if cur is not None:
                    e = block_expert(pe, cur)
                    pe.wait_ge(s_xbt, cur.i + 1)
                    wait(pe, s_hb, cur.i - 1)
                    pe.matmul(bank[2 + cur.side], xbt[:, cur.side, :], e1_sb[:, bass.ds(e * HID, HID)],
                              start=True, stop=True).then_inc(s_hps, 1)
                if prev is not None:
                    e = block_expert(pe, prev)
                    pe.wait_ge(s_hb, prev.i + 1)
                    wait(pe, s_hbt, prev.i - 1)
                    for n in range(HID // P):
                        mm = pe.transpose(bank[4 + prev.side][:, n * P:(n + 1) * P],
                                          hb[:, prev.side, n * P:(n + 1) * P], ident[:, :])
                    mm.then_inc(s_htps, 1)
                    pe.wait_ge(s_hbt, prev.i + 1)
                    wait(pe, s_yb, prev.i - 1)
                    for n in range(HID // P):
                        mm = pe.matmul(bank[6 + prev.side][:, 0:C], hbt[:, prev.side, n * P:(n + 1) * P],
                                       e2_sb[:, bass.ds(e * HID + n * C, C)],
                                       start=(n == 0), stop=(n == HID // P - 1))
                    mm.then_inc(s_yps, 1)

            walk_blocks(pe, block_step)

        @block.vector
        def _(dve):
            dve.wait_ge(s_const, CONSTS)
            dve.wait_ge(s_ld0, 16 * FIRST_LOADS)
            dve.wait_ge(s_colps, 1)
            dve.tensor_copy(cols[:, :], T[1][:, 0:ROWS]).then_inc(s_col, 1)

            def one_hot(b):
                dve.wait_ge(s_tok[b % 2], 16 * (b // 2 + 1))
                t = tok[:, (b % 2) * S:(b % 2 + 1) * S]
                wait(dve, s_y, b - 1)
                dve.tensor_scalar(onehot[:, b % 2, :], t[0:VOCAB, :], iota_p[0:VOCAB, 0:1], None, ALU.is_equal)
                wait(dve, s_res, b - 3)
                dve.tensor_scalar(notpad[:, b % 4, :], t, float(PAD), None, ALU.not_equal).then_inc(s_hot, 1)

            def source(u):
                if u.kind == "ln2":
                    return htok[:, u.b * NB:(u.b + 1) * NB, :]
                return xe[:, u.side, :, :] if u.kind == "embed" else Y[u.slot].rearrange("p (n c) -> p n c", c=C)

            def statistics(u):
                if u.kind == "ln2":
                    dve.wait_ge(s_ht, u.b + 1)
                else:
                    dve.wait_ge(s_y, u.n + 1)
                if u.kind == "embed":
                    wait(dve, s_xn, u.n - 1)
                    dve.tensor_tensor(xe[:, u.side, :, :], Y[u.slot].rearrange("p (n c) -> p n c", c=C), pe_sb[:, :, :], ALU.add).then_inc(s_xe, 1)
                    dve.wait_ge(s_xe, u.n + 1)
                src = source(u)
                for j in range(NB):
                    ins = dve.bn_stats(bns[:, u.slot, j, :], src[:, j, :])
                ins.then_inc(s_bn, 1)

            def invert_root(u):
                dve.wait_ge(s_std, u.n + 1)
                dve.reciprocal(rstd[:, u.slot, :], std[:, u.slot, :]).then_inc(s_rstd, 1)

            def aggregate(u):
                for j in range(NB):
                    ins = dve.bn_aggr(mv[:, u.slot, j, :], bns[:, u.slot, j, :])
                if u.kind == "ln1":
                    ins.then_inc(s_ag, 1)
                    dve.wait_ge(s_ag, u.b + 1)
                    var = mv[:, u.slot, :, 1]
                    ins = dve.tensor_scalar(var, var, VAR_FLOOR, None, ALU.max)
                ins.then_inc(s_var, 1)

            def normalise(u):
                dve.wait_ge(s_rstd, u.n + 1)
                if u.kind != "ln2":
                    wait(dve, s_t, u.n - 1)
                for j in range(NB):
                    src = source(u)[:, j, :]
                    dst = xf[:, u.b * NB + j, :] if u.kind == "ln2" else xn[:, u.side, j, :]
                    ins = dve.tensor_scalar(dst, src, mv[:, u.slot, j, 0:1], rstd[:, u.slot, j:j + 1],
                                            ALU.subtract, ALU.mult)
                ins.then_inc(s_xn, 1)

            def step(u, prev, _):
                if u is not None and u.kind == "embed" and u.b + 1 < B:
                    one_hot(u.b + 1)
                if u is not None:
                    statistics(u)
                    dve.wait_ge(s_bn, u.n + 1)
                if prev is not None:
                    invert_root(prev)
                if u is not None:
                    aggregate(u)
                if prev is not None:
                    normalise(prev)

            one_hot(0)
            walk(dve, step)

            dve.wait_ge(s_ldr, 16 * REST_LOADS)
            dve.wait_ge(s_scaled, 3)

            def add_v_bias(b):
                for j in range(NB):
                    dve.wait_ge(s_vps, NB * b + j + 1)
                    dve.tensor_tensor(vv[:, j, :], ps_s[j], bv_rep[:, :], ALU.add).then_inc(s_v, 1)

            def clip_exp(m):
                dve.wait_ge(s_e, m + 1)
                dve.tensor_scalar(expa, expa, 1.0 / DECAY_FLOOR - 1.0, None, ALU.min).then_inc(s_em, 1)

            def sums(m):
                dve.wait_ge(s_sp, m + 1)
                wait(dve, s_dec, m)
                dve.tensor_tensor_scan(cum, ones[:, :], soft, 0.0, ALU.mult, ALU.add).then_inc(s_scan, 1)

            def clip_sums(m):
                dve.wait_ge(s_scan, m + 1)
                wait(dve, s_inv, m)
                dve.tensor_scalar(cumc, cum, float(-np.log(INV_FLOOR)), None, ALU.min).then_inc(s_cc, 1)

            def decayed(m, pair):
                dve.wait_ge(s_qps, m + 1)
                dve.wait_ge(s_dec, m + 1)
                dve.scalar_tensor_tensor(out=qd[:, pair % 2, :], in0=ps_q, scalar=bqs[:, pair:pair + 1],
                                         in1=decay, op0=ALU.add, op1=ALU.mult).then_inc(s_q, 1)
                dve.wait_ge(s_kps, m + 1)
                dve.wait_ge(s_inv, m + 1)
                dve.scalar_tensor_tensor(out=kd[:, pair % 2, :], in0=ps_ak, scalar=cols[:, R_BK + pair:R_BK + pair + 1],
                                         in1=inv_decay, op0=ALU.add, op1=ALU.mult).then_inc(s_k, 1)

            def mask(m, c):
                dve.wait_ge(s_sps, NB * m + c + 1)
                dve.tensor_tensor(probs[:, c % 2, :, :], psum[:, 4 + c % 2 * 2:6 + c % 2 * 2, 0:P],
                                  causal[:, :].unsqueeze(1).to_broadcast([P, 2, P]), ALU.mult).then_inc(s_p, 1)

            def add_state(m, c):
                dve.wait_ge(s_stps, (NB - 1) * m + c + 1)
                if c:
                    dve.wait_ge(s_st, (NB - 1) * m + c)
                for h in range(2):
                    r = slice(h * DH, (h + 1) * DH)
                    new = ps_kso[r, 3 * P + h * DH:3 * P + (h + 1) * DH]
                    if c == 0:
                        ins = dve.tensor_copy(state[r, 0, r], new)
                    else:
                        ins = dve.tensor_tensor(state[r, c % 2, r], new, state[r, (c - 1) % 2, r], ALU.add)
                ins.then_inc(s_st, 1)

            def add_attention(b):
                dve.wait_ge(s_ops, b + 1)
                row = res[:, bass.ds(b, 1), 1:S + 1].rearrange("p a s -> p (a s)")
                dve.scalar_tensor_tensor(out=row, in0=ps_kso, scalar=cols[:, R_BOUT:R_BOUT + 1], in1=row,
                                         op0=ALU.add, op1=ALU.add).then_inc(s_h, 1)

            def attend(m, b, pair, last):
                more = not (last and pair == PAIRS - 1)
                if more:
                    clip_exp(m + 1)
                mask(m, 0)
                mask(m, 1)
                add_state(m, 0)
                if more:
                    sums(m + 1)
                mask(m, 2)
                add_state(m, 1)
                if more:
                    clip_sums(m + 1)
                mask(m, 3)
                add_state(m, 2)
                if more:
                    decayed(m + 1, (pair + 1) % PAIRS)
                if pair == PAIRS - 1:
                    if not last:
                        add_v_bias(b + 1)
                    add_attention(b)

            add_v_bias(0)
            clip_exp(0)
            sums(0)
            clip_sums(0)
            decayed(0, 0)
            with dve.Fori(0, B - 1) as b:
                for pair in range(PAIRS):
                    attend(PAIRS * b + pair, b, pair, False)
            for pair in range(PAIRS):
                attend(PAIRS * (B - 1) + pair, B - 1, pair, True)

            walk_ln2(step)
            dve.wait_ge(s_zero, 32)

            steps = [0]

            def then(ins):
                steps[0] += 1
                ins.then_inc(s_d, 1)
                dve.wait_ge(s_d, steps[0])

            def by_block(i):
                return small[:, i, :].rearrange("p (t e) -> p t e", e=EXPERTS)

            def by_expert(i):
                return small[:, i, :].rearrange("p (e t) -> p e t", e=EXPERTS)

            rank8 = ramps[:, 0:EXPERTS]
            full = ramps[:, EXPERTS:EXPERTS + TB]
            number = ramps[:, EXPERTS + TB:EXPERTS + TB + SLOT_BLOCKS]
            first8 = small[:, 1, TB:2 * TB]
            slot_f = small[:, 1, 2 * TB:3 * TB]
            count, blocks = small[:, 8, 0:8], small[:, 8, 8:16]
            end_block, start_block, shift = small[:, 8, 16:24], small[:, 8, 24:32], small[:, 8, 32:40]
            wide = [P, TB, EXPERTS]
            dve.wait_ge(s_lg, 1)
            then(dve.tensor_tensor(by_block(0), bank[6][:, 0:TB * EXPERTS].rearrange("p (t e) -> p t e", e=EXPERTS),
                                   br_rep[:, :].unsqueeze(1).to_broadcast(wide), ALU.add))
            then(dve.tensor_reduce(top, by_block(0), AX.X, ALU.max))
            then(dve.tensor_tensor(by_block(2), by_block(0), top.unsqueeze(2).to_broadcast(wide), ALU.is_ge))
            then(dve.tensor_tensor(by_block(3), by_block(2), rank8.unsqueeze(1).to_broadcast(wide), ALU.mult))
            then(dve.tensor_reduce(first8, by_block(3), AX.X, ALU.max))
            then(dve.tensor_copy(by_expert(5), rank8.unsqueeze(2).to_broadcast([P, EXPERTS, TB])))
            then(dve.tensor_tensor(by_expert(4), by_expert(5), first8.unsqueeze(1).to_broadcast([P, EXPERTS, TB]),
                                   ALU.is_equal))
            then(dve.tensor_tensor(gate_arg, top, top, ALU.subtract))
            dve.wait_ge(s_gexp, 1)
            then(dve.reciprocal(gate_inv, gate_exp))
            then(dve.tensor_tensor(gate, gate_exp, gate_inv, ALU.mult))
            dve.wait_ge(s_rank, 1)
            then(dve.tensor_copy(small[:, 5, :], bank[1][:, 0:EXPERTS * TB]))
            then(dve.tensor_tensor_scan(small[:, 6, :], ones[:, 0:EXPERTS * TB], small[:, 5, :], 0.0, ALU.mult, ALU.add))
            then(dve.tensor_tensor(small[:, 7, :], small[:, 6, :], small[:, 5, :], ALU.subtract))
            then(dve.tensor_tensor(count, by_expert(6)[:, :, TB - 1], by_expert(7)[:, :, 0], ALU.subtract))
            then(dve.tensor_tensor(by_expert(9), count.unsqueeze(2).to_broadcast([P, EXPERTS, TB]),
                                   full.unsqueeze(1).to_broadcast([P, EXPERTS, TB]), ALU.is_gt))
            then(dve.tensor_reduce(blocks, by_expert(9), AX.X, ALU.add))
            then(dve.tensor_tensor_scan(end_block, ones[:, 0:EXPERTS], blocks, 0.0, ALU.mult, ALU.add))
            then(dve.tensor_tensor(start_block, end_block, blocks, ALU.subtract))
            then(dve.scalar_tensor_tensor(out=shift, in0=start_block, scalar=float(P), in1=by_expert(7)[:, :, 0],
                                          op0=ALU.mult, op1=ALU.subtract))
            then(dve.tensor_tensor(by_expert(10), by_expert(7), shift.unsqueeze(2).to_broadcast([P, EXPERTS, TB]),
                                   ALU.add))
            then(dve.tensor_tensor(small[:, 11, :], bank[0][:, 0:EXPERTS * TB], small[:, 10, :], ALU.add))
            then(dve.tensor_tensor(small[:, 10, :], small[:, 11, :], chosen, ALU.mult))
            then(dve.tensor_reduce(slot_f, small[:, 10, :].rearrange("p (e t) -> p t e", e=EXPERTS), AX.X, ALU.add))
            then(dve.tensor_copy(slot_u[:, :], slot_f))
            assert steps[0] == SLOT_STEP
            ended = small[:, 2:4, :].rearrange("p a b -> p (a b)")[:, 0:SLOT_BLOCKS * (EXPERTS - 1)]
            ended = ended.rearrange("p (i e) -> p i e", e=EXPERTS - 1)
            narrow = [P, SLOT_BLOCKS, EXPERTS - 1]
            then(dve.tensor_tensor(ended, number.unsqueeze(2).to_broadcast(narrow),
                                   end_block[:, 0:EXPERTS - 1].unsqueeze(1).to_broadcast(narrow), ALU.is_ge))
            then(dve.tensor_reduce(small[:, 9, 0:SLOT_BLOCKS], ended, AX.X, ALU.add))
            then(dve.tensor_copy(blk_e[:, :], small[:, 9, 0:SLOT_BLOCKS]))
            assert steps[0] == DISPATCH_STEPS

            def block_step(cur, prev, _):
                if cur is not None:
                    e = block_expert(dve, cur)
                    dve.wait_ge(s_hps, cur.i + 1)
                    wait(dve, s_htps, cur.i - 1)
                    dve.tensor_tensor(hb[:, cur.side, :], bank[2 + cur.side], eb1_rep[:, bass.ds(e * HID, HID)],
                                      ALU.add).then_inc(s_hb, 1)
                if prev is not None:
                    e = block_expert(dve, prev)
                    dve.wait_ge(s_yps, prev.i + 1)
                    wait(dve, s_yst[prev.side], 16 * prev.half)
                    dve.tensor_tensor(yb[:, prev.side, :], bank[6 + prev.side][:, 0:C],
                                      eb2_rep[:, bass.ds(e * C, C)], ALU.add).then_inc(s_yb, 1)

            walk_blocks(dve, block_step)

            for b in range(B):
                dve.wait_ge(s_gat[b], 16 * NB)
                for t in range(b * NB, (b + 1) * NB):
                    ins = dve.scalar_tensor_tensor(out=htok[:, t, :], in0=xf[:, t, :], scalar=gate[:, t:t + 1],
                                                   in1=htok[:, t, :], op0=ALU.mult, op1=ALU.add)
                ins.then_inc(s_fin, 1)


_INS = ["x", "L0_tok_emb", "L0_tok_ln0_g", "L0_tok_ln0_b", "L0_tok_W1", "L0_tok_g1", "L0_tok_b1", "L0_tok_W2",
        "L0_tok_g2", "L0_tok_b2", "L0_attn_gamma", "L0_attn_w_qkv", "L0_attn_b_qkv", "L0_attn_w_a", "L0_attn_b_a",
        "L0_attn_w_out", "L0_attn_b_out", "L0_ffn_Wr", "L0_ffn_br", "L0_ffn_W1", "L0_ffn_b1", "L0_ffn_W2",
        "L0_ffn_b2"]


def _constants():
    f = np.float32
    pos = np.arange(S - 1, -1, -1, dtype=f)
    inv_freq = f(1.0) / np.power(f(10000.0), np.arange(0.0, C, 2.0, dtype=f) / f(C))
    arg = pos[:, None] * inv_freq[None, :]
    pe = np.concatenate([np.sin(arg), np.cos(arg)], axis=-1).astype(f)
    at = np.arange(P)
    ramps = np.concatenate([EXPERTS - np.arange(EXPERTS), P * np.arange(TB), np.arange(SLOT_BLOCKS)]).astype(f)
    return {"pe": pe, "identity": np.eye(P, dtype=f), "causal": (at[:, None] <= at[None, :]).astype(f),
            "before": (at[:, None] < at[None, :]).astype(f), "ramps": ramps}


def kernel(**inputs):
    import concourse.bacc as bacc
    from concourse.bass_utils import run_bass_kernel_spmd

    nc = bacc.Bacc("TRN2", target_bir_lowering=False, num_devices=1)
    arrays, args = {}, []
    given = {name: np.ascontiguousarray(inputs[name]) for name in _INS}
    for name, a in {**given, **_constants()}.items():
        arrays[f"in_{name}"] = a
        args.append(nc.dram_tensor(f"in_{name}", a.shape, mybir.dt.from_np(a.dtype), kind="ExternalInput").ap())
    out = nc.dram_tensor("out", (B, S, C), F32, kind="ExternalOutput").ap()
    tower(nc, *args, out)
    r = run_bass_kernel_spmd(nc, [arrays], core_ids=[0])
    return r.results[0]["out"]
```

```python
from contextlib import ExitStack

import numpy as np

import concourse.bass as bass
from concourse import mybir

F32 = mybir.dt.float32
F32R = mybir.dt.float32r
I32 = mybir.dt.int32
U32 = mybir.dt.uint32
ALU = mybir.AluOpType
ACT = mybir.ActivationFunctionType
AX = mybir.AxisListType

P = 128
B, S, C = 8, 512, 128
NB = S // P
LAYERS, VOCAB, PAD = 8, 33, 1
HEADS, DH = 8, 64
DI = HEADS * DH
PAIRS = HEADS // 2
EXPERTS, HID = 8, 512
TB = B * NB
RING, AHEAD = 8, 5
SLOT_BLOCKS = -(-((B * S + EXPERTS * (P - 1)) // P) // RING) * RING

EPS_EMB, EPS_CONV, EPS_LN = 1e-12, 1e-5, 1e-5
VAR_FLOOR = 1e-24 * EPS_LN / C
DECAY_FLOOR, INV_FLOOR = 1e-10, 1e-8
Q_SCALE = DH ** -0.5

R_G2, R_B2, R_G1, R_B1 = 0, LAYERS + 1, 2 * (LAYERS + 1), 3 * LAYERS + 2
R_GAMMA = R_B1 + LAYERS
R_BOUT, R_BQ = R_GAMMA + 1, R_GAMMA + 2
R_BK, R_BA = R_BQ + PAIRS, R_BQ + 2 * PAIRS
ROWS = R_BA + PAIRS
RAMPS = EXPERTS + TB + SLOT_BLOCKS + P

U_CONV = B
U_LN1 = U_CONV + 2 * B * LAYERS
U_LN2 = U_LN1 + B
UNITS = U_LN2 + B


class Unit:

    def __init__(self, kind, b, n, n0, layer=0):
        self.kind, self.b, self.n, self.n0, self.layer = kind, b, n, n0, layer

    @property
    def slot(self):
        return self.n0 % 4

    @property
    def side(self):
        return self.n0 % 2

    @property
    def update(self):
        return self.b if self.kind == "embed" else B + B * self.layer + self.b


def conv_unit(which, layer, b):
    n = U_CONV + 2 * B * layer + (B if which == "conv2" else 0) + b
    return Unit(which, b, n, (B if which == "conv2" else 0) + b, layer)


def head_units():
    return [Unit("embed", b, b, b) for b in range(B)] + [conv_unit("conv1", 0, b) for b in (0, 1)]


def layer_units(l):
    return ([conv_unit("conv1", l, b) for b in range(2, B)] + [conv_unit("conv2", l, b) for b in range(B)]
            + [conv_unit("conv1", l + 1, b) for b in (0, 1)])


def tail_units():
    return layer_units(LAYERS - 1)[:-2] + [Unit("ln1", b, U_LN1 + b, b) for b in range(B)]


def ln2_units():
    return [Unit("ln2", b, U_LN2 + b, b) for b in range(B)]


def walk(eng, step):
    def run(units, before):
        chain = before + units
        for i in range(2, len(chain)):
            step(chain[i], chain[i - 1], chain[i - 2])

    run(head_units(), [None, None])
    with eng.Fori(0, LAYERS - 1) as l:
        run(layer_units(l), [conv_unit("conv1", l, 0), conv_unit("conv1", l, 1)])
    run(tail_units() + [None, None], [conv_unit("conv1", LAYERS - 1, 0), conv_unit("conv1", LAYERS - 1, 1)])


POOL_BLOCKS = 1
EARLY = 2


def ln2_steps():
    chain = [None] * 3 + ln2_units() + [None] * 3
    return [[chain[i - k] for k in range(4)] for i in range(3, len(chain))]


class Block:

    def __init__(self, i, slot, turn):
        self.i, self.slot, self.side, self.turn = i, slot, slot % 2, turn


def walk_blocks(eng, step):
    def static(i):
        return lambda d: Block(i + d, (i + d) % RING, (i + d) // RING) if 0 <= i + d < SLOT_BLOCKS else None

    first = RING + 1
    turns = (SLOT_BLOCKS - AHEAD - first) // RING
    for i in range(-AHEAD, first):
        step(static(i), i == -AHEAD, i == first - 1)
    with eng.Fori(0, turns) as r:
        for k in range(first, first + RING):
            step(lambda d: Block(RING * r + k + d, (k + d) % RING, r + (k + d) // RING),
                 k == first, k == first + RING - 1)
    for i in range(first + RING * turns, SLOT_BLOCKS + 1):
        step(static(i), i == first + RING * turns, i == SLOT_BLOCKS)


def tower(nc, x, emb, ln0_g, ln0_b, W1, g1, b1, W2, g2, b2, gamma, w_qkv, b_qkv, w_a, b_a, w_out, b_out,
          Wr, br, E1, eb1, E2, eb2, pe, ident_in, causal_in, before_in, ramps_in, out):
    with ExitStack() as ctx:
        def sb(name, shape, dt=F32):
            return ctx.enter_context(nc.sbuf_tensor(name, shape, dt))

        def sem(name):
            return ctx.enter_context(nc.semaphore(name))

        ident = sb("ident", [P, P])
        causal = sb("causal", [P, P])
        before = sb("before", [P, P])
        ones = sb("ones", [P, S])
        ramps = sb("ramps", [P, RAMPS])
        table = sb("table", [ROWS, C])
        cols = sb("cols", [P, ROWS])
        nba = sb("nba", [P, PAIRS])
        bqs = sb("bqs", [P, PAIRS])
        eps_emb = sb("eps_emb", [P, 1])
        eps_conv = sb("eps_conv", [P, 1])
        zero_col = sb("zero_col", [P, 1])
        iota_p = sb("iota_p", [P, 1])
        exp_probe = sb("exp_probe", [P, 1])
        emb_sb = sb("emb_sb", [VOCAB, C])
        pe_sb = sb("pe_sb", [P, NB, C])
        onehot = sb("onehot", [VOCAB, 2, S])
        w_conv = sb("w_conv", [P, 2, LAYERS * 3, C])
        wqkv_sb = sb("wqkv_sb", [P, 3 * DI])
        wa_sb = sb("wa_sb", [P, DI])
        wout_sb = sb("wout_sb", [P, PAIRS, C])
        bv_rep = sb("bv_rep", [P, DI])
        wr_sb = sb("wr_sb", [P, EXPERTS])
        br_rep = sb("br_rep", [P, EXPERTS])
        e1_sb = sb("e1_sb", [P, EXPERTS * HID])
        e2_sb = sb("e2_sb", [P, EXPERTS * HID // P * C])
        eb1_rep = sb("eb1_rep", [P, EXPERTS * HID])
        eb2_rep = sb("eb2_rep", [P, EXPERTS * C])

        res = sb("res", [P, B, S + 2])
        bns = sb("bns", [P, 4, NB, 6])
        mv = sb("mv", [P, 4, NB, 2])
        std = sb("std", [P, 4, NB])
        rstd = sb("rstd", [P, 4, NB])
        xn = sb("xn", [P, 2, NB, C])
        delta = sb("delta", [P, 2, S])

        xs = sb("xs", [P, S])
        kd = sb("kd", [P, 2, S])
        kn = sb("kn", [P, NB - 1, P])
        vv = sb("vv", [P, NB, DI])
        probs = sb("probs", [P, 2, 2, P])
        state = sb("state", [P, 2, P])
        att = sb("att", [P, PAIRS, S])

        htok = w_conv[:, :, :, :].rearrange("p w k c -> p (w k) c")[:, 0:TB, :]
        small = sb("small", [P, 12, EXPERTS * TB])
        ids = sb("ids", [P, TB])
        slot_u = sb("slot_u", [P, 2, TB], U32)
        blk_e = sb("blk_e", [P, SLOT_BLOCKS], I32)
        slot_row = sb("slot_row", [P, 4, SLOT_BLOCKS])
        gate_parts = sb("gate_parts", [P, 2, TB], F32R)
        idx = sb("idx", [P, 2, RING], U32)
        xh = vv[:, :, :].rearrange("p a s -> p (a s)").rearrange("p (r c) -> p r c", r=RING)
        ob = kd[:, :, :].rearrange("p a s -> p (a s)").rearrange("p (r c) -> p r c", r=RING)
        xbt, yb = (delta[:, i, 0:2 * C].rearrange("p (a c) -> p a c", c=C) for i in range(2))
        hb, hbt = att[:, 0:2, :], att[:, 2:4, :]

        late = ExitStack()

        def sbl(name, shape):
            return late.enter_context(nc.sbuf_tensor(name, shape, F32))

        mid = sbl("mid", [P, B, S + 2])
        arena = sbl("arena", [P, 8, S])
        expa, soft, cum, cumc, decay, inv_decay = (arena[:, i, :] for i in range(6))
        qd = arena[:, 6:8, :]
        xf = arena[:, :, :].rearrange("p a (n c) -> p (a n) c", c=C)
        tok = arena[:, :, :].bitcast(I32)
        late.close()
        place = sb("place", [P, TB, P], F32R)
        held = sb("held", [P, TB, 3, SLOT_BLOCKS], F32R)

        rows_dram = nc.dram_tensor("rows_dram", [B * S + 1, 2 * C], F32, kind="Internal").ap()

        psum = ctx.enter_context(nc.psum_tensor("psum", [P, 8, 512], F32))
        bank = [psum[:, i, :] for i in range(8)]
        Y = bank[0:4]
        T = bank[4:6]
        ps_ak, ps_q, ps_kso, ps_o = bank[0:4]
        ps_s = bank[4:8]
        ps_out = ps_s[3]

        top = small[:, 1, 0:TB]
        gate_arg, gate_exp = small[:, 1, 3 * TB:4 * TB], small[:, 1, 4 * TB:5 * TB]
        gate_inv, gate = small[:, 1, 5 * TB:6 * TB], small[:, 1, 6 * TB:7 * TB]
        in_slot_block = res[:, :, :].rearrange("p b s -> p (b s)")[:, 0:TB * SLOT_BLOCKS].rearrange(
            "p (t k) -> p t k", t=TB)
        PLACES = 8
        chosen = small[:, 4, :]

        s_tok = [sem(f"tokens_loaded_{r}") for r in range(B)]
        s_lde = sem("embedding_loaded")
        s_ldt = sem("table_loaded")
        s_ldw = [sem("first_layer_loaded"), sem("conv_weights_loaded")]
        s_ldr = sem("rest_loaded")
        s_const = sem("constants_made")
        s_small = sem("zeros_made")
        s_colps = sem("columns_turned")
        s_col = sem("columns_ready")
        s_scaled = sem("q_weights_scaled")
        s_hot = sem("onehot_ready")
        s_mask = sem("padding_found")
        s_y = sem("y_ready")
        s_bn = sem("bn_stats_done")
        s_ag = sem("aggregated")
        s_var = sem("var_ready")
        s_std = sem("std_ready")
        s_rstd = sem("rstd_ready")
        s_xn = sem("xn_ready")
        s_xnp = sem("xn_pool_part_ready")
        s_t = sem("t_ready")
        s_aff = sem("affine_done")
        s_res = sem("residual_updated")
        s_ht = sem("htok_copied")

        s_xs = sem("row_staged")
        s_aps, s_qps, s_kps = sem("a_projected"), sem("q_projected"), sem("k_projected")
        s_e, s_em, s_sp, s_scan = sem("exp_done"), sem("exp_clipped"), sem("softplus_done"), sem("scan_done")
        s_cc, s_dec, s_inv = sem("cum_clipped"), sem("decay_ready"), sem("inv_decay_ready")
        s_q, s_k = sem("q_ready"), sem("k_ready")
        s_vps, s_v = sem("v_projected"), sem("v_ready")
        s_knps, s_kn = sem("k_turned"), sem("kn_ready")
        s_sps, s_p = sem("scores_ready"), sem("probs_ready")
        s_stps, s_st = sem("state_product_ready"), sem("state_ready")
        s_pv = sem("chunk_output_ready")
        s_att = sem("att_ready")
        s_ops, s_h = sem("out_projected"), sem("attention_added")

        s_lg = sem("logits_ready")
        s_d = sem("dispatch_step")
        s_gexp = sem("gate_exp_done")
        s_rank = sem("ranks_ready")
        s_ids = sem("ids_ready")
        s_rows = sem("rows_stored")
        s_hg = sem("held_gates_ready")
        s_slots = sem("slots_filled")
        s_gcol = sem("gates_ready")
        s_idx = sem("idx_ready")
        s_turns = sem("waits_of_pool")
        s_xh = [sem(f"block_gathered_{r}") for r in range(RING)]
        s_xbps, s_xbt = sem("block_turned"), sem("xbt_ready")
        s_hps, s_hb = sem("hidden_ready"), sem("hidden_biased")
        s_htps, s_hbt = sem("hidden_turned"), sem("hbt_ready")
        s_yps, s_yb, s_ob = sem("expert_out_ready"), sem("yb_ready"), sem("ob_ready")
        s_sc = [sem(f"block_scattered_{r}") for r in range(RING)]

        block = ctx.enter_context(nc.Block())

        def wait(eng, s, value):
            if not isinstance(value, int) or value > 0:
                eng.wait_ge(s, value)

        CONSTS = 10
        EMB_LOADS, TABLE_LOADS, REST_LOADS = 3, 10, 13
        CHOSEN_STEP, GATE_STEP, BLOCK_STEP, PLACE_STEP, DISPATCH_STEPS = 7, 8, 30, 32, 41

        def block_expert(eng, blk):
            if blk is not None:
                return eng.value_load(blk_e[0:1, bass.ds(blk.i, 1)], min_val=0, max_val=EXPERTS - 1)

        @block.sync
        def _(sp):
            def load_tokens(b):
                sp.dma_start(tok[:, b, :], x[b].partition_broadcast(P)).then_inc(s_tok[b], 16)

            def load_convs(layers, done):
                for i, w in enumerate((W1, W2)):
                    sp.dma_start(w_conv[:, i, 3 * layers.start:3 * layers.stop, :],
                                 w[layers].rearrange("l k i o -> i (l k) o")).then_inc(done, 16)

            load_tokens(0)
            sp.dma_start(emb_sb[:, :], emb).then_inc(s_lde, 16)
            sp.dma_start(pe_sb[:, :, :], pe.rearrange("(n p) c -> p n c", p=P)).then_inc(s_lde, 16)
            sp.dma_start(ident[:, :], ident_in).then_inc(s_lde, 16)
            load_tokens(1)
            for r, src in ((R_G2, ln0_g), (R_B2, ln0_b), (R_GAMMA, gamma), (R_BOUT, b_out)):
                sp.dma_start(table[r:r + 1, :], src.rearrange("(a c) -> a c", a=1)).then_inc(s_ldt, 16)
            for r, src in ((R_G2 + 1, g2), (R_B2 + 1, b2), (R_G1, g1), (R_B1, b1)):
                sp.dma_start(table[r:r + LAYERS, :], src).then_inc(s_ldt, 16)
            sp.dma_start(table[R_BQ:R_BQ + 2 * PAIRS, :],
                         b_qkv[0:2 * DI].rearrange("(a c) -> a c", c=C)).then_inc(s_ldt, 16)
            sp.dma_start(table[R_BA:R_BA + PAIRS, :], b_a.rearrange("(a c) -> a c", c=C)).then_inc(s_ldt, 16)
            for b in (2, 3):
                load_tokens(b)
            load_convs(slice(0, 1), s_ldw[0])
            for b in range(4, B):
                load_tokens(b)
            load_convs(slice(1, LAYERS), s_ldw[1])
            sp.dma_start(causal[:, :], causal_in).then_inc(s_ldr, 16)
            sp.dma_start(before[:, :], before_in).then_inc(s_ldr, 16)
            sp.dma_start(ramps[:, :], ramps_in.partition_broadcast(P)).then_inc(s_ldr, 16)
            sp.dma_start(wqkv_sb[:, :], w_qkv).then_inc(s_ldr, 16)
            sp.dma_start(wa_sb[:, :], w_a).then_inc(s_ldr, 16)
            sp.dma_start(wout_sb[:, :, :], w_out.rearrange("(h p) c -> p h c", p=P)).then_inc(s_ldr, 16)
            sp.dma_start(bv_rep[:, :], b_qkv[2 * DI:3 * DI].partition_broadcast(P)).then_inc(s_ldr, 16)
            sp.dma_start(wr_sb[:, :], Wr).then_inc(s_ldr, 16)
            sp.dma_start(br_rep[:, :], br.partition_broadcast(P)).then_inc(s_ldr, 16)
            sp.dma_start(e1_sb[:, :].rearrange("p (e h) -> p e h", e=EXPERTS),
                         E1.rearrange("e c h -> c e h")).then_inc(s_ldr, 16)
            sp.dma_start(e2_sb[:, :].rearrange("p (a c) -> p a c", c=C),
                         E2.rearrange("e (n p) c -> p (e n) c", p=P)).then_inc(s_ldr, 16)
            sp.dma_start(eb1_rep[:, :], eb1.rearrange("e h -> (e h)").partition_broadcast(P)).then_inc(s_ldr, 16)
            sp.dma_start(eb2_rep[:, :], eb2.rearrange("e c -> (e c)").partition_broadcast(P)).then_inc(s_ldr, 16)
            sp.wait_ge(s_small, 1)
            sp.dma_start(rows_dram[B * S:B * S + 1, :], small[0:1, 0, 0:2 * C]).then_inc(s_rows, 16)

            for b in range(B):
                sp.wait_ge(s_ht, b + 1)
                here = rows_dram[b * S:(b + 1) * S, :].rearrange("(n p) c -> p n c", p=P)
                sp.dma_start(here[:, :, C:2 * C], htok[:, b * NB:(b + 1) * NB, :]).then_inc(s_rows, 16)
                sp.wait_ge(s_xn, U_LN2 + b + 1)
                sp.wait_ge(s_xnp, b + 1)
                sp.dma_start(here[:, :, 0:C], xf[:, b * NB:(b + 1) * NB, :]).then_inc(s_rows, 16)

        @block.gpsimd
        def _(pool):
            pool.memset(eps_emb[:, :], EPS_EMB).then_inc(s_const, 1)
            pool.memset(eps_conv[:, :], EPS_CONV).then_inc(s_const, 1)
            pool.memset(zero_col[:, :], 0.0).then_inc(s_const, 1)
            pool.memset(ones[:, :], 1.0).then_inc(s_const, 1)
            pool.memset(state[:, :, :], 0.0).then_inc(s_const, 1)
            for buf in (res, mid):
                for edge in (0, S + 1):
                    pool.memset(buf[:, :, edge:edge + 1], 0.0).then_inc(s_const, 1)
            pool.iota(iota_p[:, :], [[0, 1]], base=0, channel_multiplier=1,
                      allow_small_or_imprecise_dtypes=True).then_inc(s_const, 1)
            pool.memset(small[:, 0, :], 0.0).then_inc(s_small, 1)

            def step(u, _, lag):
                if lag is None or lag.kind not in ("embed", "conv2"):
                    return
                row = res[:, lag.b, 1:S + 1]
                if lag.kind == "embed":
                    pool.wait_ge(s_tok[lag.b], 16)
                    pool.tensor_scalar(vv[:, lag.b % NB, :], tok[:, lag.b, :], float(PAD), 1.0,
                                       ALU.is_equal, ALU.is_lt).then_inc(s_mask, 1)
                    pool.wait_ge(s_mask, lag.b + 1)
                pool.wait_ge(s_aff, lag.n + 1)
                if lag.kind == "embed":
                    pool.tensor_tensor(row, delta[:, lag.side, :], vv[:, lag.b % NB, :], ALU.mult).then_inc(s_res, 1)
                else:
                    pool.tensor_tensor(row, row, delta[:, lag.side, :], ALU.add).then_inc(s_res, 1)

            walk(pool, step)

            pool.wait_ge(s_ldr, 16 * REST_LOADS)
            pool.wait_ge(s_col, 1)
            pool.tensor_scalar(wqkv_sb[:, 0:DI], wqkv_sb[:, 0:DI], Q_SCALE, None, ALU.mult).then_inc(s_scaled, 1)
            pool.tensor_scalar(bqs[:, :], cols[:, R_BQ:R_BQ + PAIRS], Q_SCALE, None, ALU.mult).then_inc(s_scaled, 1)
            pool.tensor_scalar(nba[:, :], cols[:, R_BA:R_BA + PAIRS], -1.0, None, ALU.mult).then_inc(s_scaled, 1)
            pool.tensor_scalar(ids[:, :], ramps[:, EXPERTS:EXPERTS + TB], iota_p[:, 0:1], 1.0, ALU.add,
                               ALU.add).then_inc(s_ids, 1)

            def settle():
                pool.sem_inc(s_turns, 1)

            def stage_row(b):
                pool.tensor_copy(xs[:, :], mid[:, b, 1:S + 1]).then_inc(s_xs, 1)

            pool.wait_ge(s_aff, U_LN1 + 1)
            stage_row(0)
            pool.wait_ge(s_aff, U_LN1 + B)
            for b in range(1, B):
                pool.wait_ge(s_kps, PAIRS * b)
                stage_row(b)

            for u, *_ in ln2_steps()[:B]:
                pool.wait_ge(s_ht, u.b + 1)
                pool.wait_ge(s_rstd, u.n + 1)
                for j in range(NB - POOL_BLOCKS, NB):
                    t = u.b * NB + j
                    ins = pool.tensor_scalar(xf[:, t, :], htok[:, t, :], mv[:, u.slot, j, 0:1], rstd[:, u.slot, j:j + 1],
                                             ALU.subtract, ALU.mult)
                ins.then_inc(s_xnp, 1)

            pool.wait_ge(s_rows, 16 * (2 * B + 1))

            def block_step(blk, *_):
                new, old = blk(AHEAD), blk(-1)
                if new is not None:
                    wait(pool, s_ob, new.i - RING + 1)
                    pool.wait_ge(s_idx, new.i + 1)
                    settle()
                    pool.indirect_dma_start(out=xh[:, new.slot, :], out_offset=None, in_=rows_dram,
                                            in_offset=bass.IndirectOffsetOnAxis(ap=idx[:, 0, new.slot:new.slot + 1], axis=0)
                                            ).then_inc(s_xh[new.slot], 16)
                if old is not None:
                    pool.wait_ge(s_ob, old.i + 1)
                    settle()
                    pool.indirect_dma_start(out=out_rows,
                                            out_offset=bass.IndirectOffsetOnAxis(ap=idx[:, 1, old.slot:old.slot + 1], axis=0),
                                            in_=ob[:, old.slot, :], in_offset=None, bounds_check=B * S - 1,
                                            oob_is_err=False).then_inc(s_sc[old.slot], 16)

            pool.wait_ge(s_d, BLOCK_STEP)
            for t in range(0, TB, PLACES):
                some = slice(t, t + PLACES)
                for part in range(2):
                    pool.tensor_tensor(held[:, some, 1 + part, :], in_slot_block[:, some, :],
                                       gate_parts[:, part, some].unsqueeze(2).to_broadcast([P, PLACES, SLOT_BLOCKS]),
                                       ALU.mult).then_inc(s_hg, 1)

            out_rows = out.rearrange("b s c -> (b s) c")
            walk_blocks(pool, block_step)
            for r in range(RING):
                pool.wait_ge(s_sc[r], 16 * (SLOT_BLOCKS // RING))

        @block.scalar
        def _(act):
            act.wait_ge(s_const, CONSTS)

            def root(u):
                eps = {"embed": eps_emb, "ln1": zero_col}.get(u.kind, eps_conv)
                act.activation(std[:, u.slot, :], mv[:, u.slot, :, 1], ACT.Sqrt, bias=eps[:, 0:1]).then_inc(s_std, 1)

            def affine(u):
                src = T[u.side][:, :]
                row = mid[:, u.b, 1:S + 1]
                if u.kind == "conv1":
                    act.activation(row, src, ACT.Relu, bias=cols[:, bass.ds(R_B1 + u.layer, 1)],
                                   scale=cols[:, bass.ds(R_G1 + u.layer, 1)]).then_inc(s_aff, 1)
                elif u.kind in ("embed", "conv2"):
                    k = 0 if u.kind == "embed" else u.layer + 1
                    act.activation(delta[:, u.side, :], src, ACT.Identity, bias=cols[:, bass.ds(R_B2 + k, 1)],
                                   scale=cols[:, bass.ds(R_G2 + k, 1)]).then_inc(s_aff, 1)
                elif u.kind == "ln1":
                    act.activation(row, src, ACT.Copy, scale=cols[:, R_GAMMA:R_GAMMA + 1]).then_inc(s_aff, 1)
                else:
                    act.activation(row, src, ACT.Copy).then_inc(s_aff, 1)

            def waits(u, lag):
                if u is not None:
                    act.wait_ge(s_var, u.n + 1)
                if lag is not None:
                    if lag.kind == "embed":
                        act.wait_ge(s_col, 1)
                    act.wait_ge(s_t, lag.n + 1)
                    if lag.kind in ("embed", "conv2"):
                        wait(act, s_res, lag.update - 1)

            def step(u, _, lag):
                waits(u, lag)
                if u is not None:
                    root(u)
                if lag is not None:
                    affine(lag)

            walk(act, step)
            act.activation(exp_probe[:, :], zero_col[:, :], ACT.Exp)

            def exp_logits(m, pair):
                act.wait_ge(s_aps, m + 1)
                wait(act, s_sp, m)
                act.activation(expa, ps_ak, ACT.Exp, bias=nba[:, pair:pair + 1], scale=-1.0).then_inc(s_e, 1)

            def softplus(m):
                act.wait_ge(s_em, m + 1)
                wait(act, s_scan, m)
                act.activation(soft, expa, ACT.Ln, bias=ones[:, 0:1]).then_inc(s_sp, 1)

            def decays(m):
                act.wait_ge(s_scan, m + 1)
                wait(act, s_q, m)
                act.activation(decay, cum, ACT.Exp, scale=-1.0).then_inc(s_dec, 1)
                act.wait_ge(s_cc, m + 1)
                wait(act, s_k, m)
                act.activation(inv_decay, cumc, ACT.Exp).then_inc(s_inv, 1)

            def take_output(m, pair):
                act.wait_ge(s_pv, NB * (m + 1))
                act.activation(att[:, pair, :], ps_o[:, :], ACT.Copy).then_inc(s_att, 1)

            def attend(m, pair, first, last):
                if not last:
                    exp_logits(m + 1, (pair + 1) % PAIRS)
                if pair == 0 and not first:
                    take_output(m - 1, PAIRS - 1)
                if not last:
                    softplus(m + 1)
                if pair:
                    take_output(m - 1, pair - 1)
                if not last:
                    decays(m + 1)

            act.wait_ge(s_scaled, 3)
            exp_logits(0, 0)
            softplus(0)
            decays(0)
            for pair in range(PAIRS):
                attend(pair, pair, pair == 0, False)
            with act.Fori(1, B - 1) as b:
                for pair in range(PAIRS):
                    attend(b * PAIRS + pair, pair, False, False)
            for pair in range(PAIRS):
                attend((B - 1) * PAIRS + pair, pair, False, pair == PAIRS - 1)

            def take_row(u):
                act.wait_ge(s_y, u.n + 1)
                act.activation(htok[:, u.b * NB:(u.b + 1) * NB, :],
                               Y[u.slot].rearrange("p (n c) -> p n c", c=C), ACT.Copy).then_inc(s_ht, 1)

            def step2(u, _, lag, __):
                if u is not None and EARLY <= u.b + 1 < B:
                    take_row(ln2_units()[u.b + 1])
                waits(u, lag)
                if u is not None:
                    root(u)
                if lag is not None:
                    affine(lag)

            for u, *_ in ln2_steps()[:EARLY]:
                take_row(u)
            take_output(B * PAIRS - 1, PAIRS - 1)
            for units in ln2_steps():
                step2(*units)

            act.wait_ge(s_d, GATE_STEP)
            act.activation(gate_exp, gate_arg, ACT.Exp).then_inc(s_gexp, 1)

            def block_step(blk, *_):
                x, h = blk(2), blk(0)
                if x is not None:
                    act.wait_ge(s_xbps, x.i + 1)
                    wait(act, s_hps, x.i - 1)
                    act.activation(xbt[:, x.side, :], bank[x.side][:, 0:P], ACT.Copy).then_inc(s_xbt, 1)
                if h is not None:
                    act.wait_ge(s_htps, h.i + 1)
                    wait(act, s_yps, h.i - 1)
                    act.activation(hbt[:, h.side, :], bank[4 + h.side], ACT.Relu).then_inc(s_hbt, 1)

            walk_blocks(act, block_step)

        @block.tensor
        def _(pe):
            def keep_warm(products, into=bank[3]):
                for _ in range(products):
                    pe.matmul(into, ones[:, 0:P], ones[:, :], start=True, stop=True)

            pe.wait_ge(s_const, CONSTS)
            keep_warm(5)
            pe.wait_ge(s_lde, 16 * EMB_LOADS)

            def produce(u):
                y = Y[u.slot]
                if u.kind == "ln2":
                    wait(pe, s_ht, u.b - 3)
                else:
                    wait(pe, s_xn, u.n - 3)
                if u.kind == "embed":
                    pe.wait_ge(s_hot, u.b + 1)
                    for j in range(NB):
                        pe.matmul(y[:, j * C:(j + 1) * C], onehot[:, u.b % 2, j * P:(j + 1) * P],
                                  emb_sb[:, :], start=True, stop=False)
                        mm = pe.matmul(y[:, j * C:(j + 1) * C], ident[:, :], pe_sb[:, j, :], start=False, stop=True)
                elif u.kind in ("conv1", "conv2"):
                    if u.kind == "conv1":
                        pe.wait_ge(s_res, B * u.layer + u.b + 1)
                    else:
                        pe.wait_ge(s_aff, u.n - B + 1)
                    src = res if u.kind == "conv1" else mid
                    which = 0 if u.kind == "conv1" else 1
                    for j in range(NB):
                        for k in range(3):
                            mm = pe.matmul(y[:, j * C:(j + 1) * C], src[:, u.b, j * P + k:j * P + k + P],
                                           w_conv[:, which, bass.ds(u.layer * 3 + k, 1), :],
                                           start=(k == 0), stop=(k == 2))
                else:
                    if u.kind == "ln1":
                        pe.wait_ge(s_res, B * LAYERS + u.b + 1)
                    else:
                        pe.wait_ge(s_h, u.b + 1)
                    for j in range(NB):
                        mm = pe.transpose(y[:, j * C:(j + 1) * C], res[:, u.b, 1 + j * P:1 + (j + 1) * P],
                                          ident[:, :])
                mm.then_inc(s_y, 1)

            def turn(u):
                if u.kind == "embed" and u.b == 1:
                    pe.wait_ge(s_col, 1)
                pe.wait_ge(s_xn, u.n + 1)
                if u.kind == "ln2":
                    pe.wait_ge(s_xnp, u.b + 1)
                wait(pe, s_aff, u.n - 1)
                for j in range(NB):
                    src = xf[:, u.b * NB + j, :] if u.kind == "ln2" else xn[:, u.side, j, :]
                    mm = pe.transpose(T[u.side][:, j * P:(j + 1) * P], src, ident[:, :])
                mm.then_inc(s_t, 1)

            def step(u, _, lag):
                if u is not None:
                    if u.kind == "conv1":
                        pe.wait_ge(s_ldw[0 if isinstance(u.n, int) and u.n < UNITS // 2 else 1], 32)
                    produce(u)
                    if u.n0 == 0 and u.kind == "embed":
                        pe.wait_ge(s_ldt, 16 * TABLE_LOADS)
                        pe.transpose(T[1][:, 0:ROWS], table[:, :], ident[0:ROWS, 0:ROWS]).then_inc(s_colps, 1)
                if lag is not None:
                    turn(lag)
                    if lag.kind == "ln1" and B // 2 <= lag.b < B - 1:
                        keep_warm(1, bank[7])

            walk(pe, step)

            pe.wait_ge(s_ldr, 16 * REST_LOADS)
            pe.wait_ge(s_scaled, 3)
            pe.wait_ge(s_xn, U_LN2)

            def project_v(b, j):
                pe.wait_ge(s_xs, b + 1)
                pe.matmul(ps_s[j], xs[:, j * P:(j + 1) * P], wqkv_sb[:, 2 * DI:3 * DI],
                          start=True, stop=True).then_inc(s_vps, 1)

            def project_aq(m, b, pair):
                f = slice(pair * P, (pair + 1) * P)
                pe.wait_ge(s_xs, b + 1)
                wait(pe, s_k, m)
                pe.matmul(ps_ak, wa_sb[:, f], xs[:, :], start=True, stop=True).then_inc(s_aps, 1)
                wait(pe, s_q, m)
                pe.matmul(ps_q, wqkv_sb[:, f], xs[:, :], start=True, stop=True).then_inc(s_qps, 1)

            def project_k(m, pair):
                pe.wait_ge(s_e, m + 1)
                pe.matmul(ps_ak, wqkv_sb[:, DI + pair * P:DI + (pair + 1) * P], xs[:, :],
                          start=True, stop=True).then_inc(s_kps, 1)

            def attend(m, b, pair, last, next_aq):
                side = pair % 2

                def chunk(c):
                    return slice(c * P, (c + 1) * P)

                def scores(c):
                    if c >= 2:
                        pe.wait_ge(s_p, NB * m + c - 1)
                    for h in range(2):
                        rows = slice(h * DH, (h + 1) * DH)
                        mm = pe.matmul(ps_s[c % 2 * 2 + h][:, 0:P], kd[rows, side, chunk(c)],
                                       qd[rows, side, chunk(c)], start=True, stop=True)
                    mm.then_inc(s_sps, 1)

                def state_product(c):
                    if c == 0:
                        pe.wait_ge(s_kn, m + 1)
                    pe.matmul(ps_kso[:, 3 * P:4 * P], kn[:, c, :], vv[:, c, pair * P:(pair + 1) * P],
                              start=True, stop=True).then_inc(s_stps, 1)

                def from_state(c):
                    pe.wait_ge(s_st, (NB - 1) * m + c)
                    pe.matmul(ps_o[:, chunk(c)], state[:, (c - 1) % 2, :], qd[:, side, chunk(c)],
                              start=True, stop=False, skip_group_check=True)

                def from_chunk(c):
                    pe.wait_ge(s_p, NB * m + c + 1)
                    for h in range(2):
                        v = vv[:, c, pair * P + h * DH:pair * P + (h + 1) * DH]
                        mm = pe.matmul(ps_o[h * DH:(h + 1) * DH, chunk(c)], v, probs[:, c % 2, h, :],
                                       start=(c == 0), stop=True, skip_group_check=True)
                    mm.then_inc(s_pv, 1)

                pe.wait_ge(s_k, m + 1)
                for c in range(NB - 1):
                    mm = pe.transpose(ps_kso[:, chunk(c)], kd[:, side, chunk(c)], ident[:, :])
                mm.then_inc(s_knps, 1)
                pe.wait_ge(s_q, m + 1)
                if pair == 0:
                    pe.wait_ge(s_v, NB * (b + 1))
                scores(0)
                scores(1)
                if not (last and pair == PAIRS - 1):
                    project_k(m + 1, (pair + 1) % PAIRS)
                if pair:
                    pe.wait_ge(s_att, m)
                from_chunk(0)
                state_product(0)
                scores(2)
                from_state(1)
                state_product(1)
                from_chunk(1)
                scores(3)
                from_state(2)
                state_product(2)
                from_chunk(2)
                if next_aq is not None:
                    next_aq()
                from_state(3)
                from_chunk(3)

            def project_out(b):
                pe.wait_ge(s_att, PAIRS * (b + 1))
                for pair in range(PAIRS):
                    mm = pe.matmul(ps_out, wout_sb[:, pair, :], att[:, pair, :],
                                   start=(pair == 0), stop=(pair == PAIRS - 1))
                mm.then_inc(s_ops, 1)

            project_aq(0, 0, 0)
            pe.wait_ge(s_aff, U_LN2)
            for j in range(NB):
                project_v(0, j)
            project_k(0, 0)
            keep_warm(1)
            project_aq(1, 0, 1)

            def early_ln2():
                for u, *_ in ln2_steps()[:EARLY]:
                    produce(u)

            def row(b, last):
                for pair in range(PAIRS):
                    m = PAIRS * b + pair
                    if pair < 2:
                        attend(m, b, pair, last, lambda: project_aq(m + 2, b, pair + 2))
                    elif last and pair == PAIRS - 1:
                        attend(m, b, pair, last, early_ln2)
                    elif not last:
                        attend(m, b, pair, last, lambda: project_aq(m + 2, b + 1, pair - 2))
                    else:
                        attend(m, b, pair, last, None)
                    if pair == PAIRS - 1:
                        if not last:
                            project_v(b + 1, 0)
                            project_v(b + 1, 1)
                        project_out(b)
                        if not last:
                            project_v(b + 1, 2)
                            pe.wait_ge(s_h, b + 1)
                            project_v(b + 1, 3)

            with pe.Fori(0, B - 1) as b:
                row(b, False)
            row(B - 1, True)

            def logits(u):
                pe.wait_ge(s_aff, u.n + 1)
                for t in range(u.b * NB, (u.b + 1) * NB):
                    mm = pe.matmul(bank[6][:, t * EXPERTS:(t + 1) * EXPERTS],
                                   mid[:, u.b, 1 + t % NB * P:1 + (t % NB + 1) * P], wr_sb[:, :], start=True, stop=True)
                mm.then_inc(s_lg, 1)

            def step2(u, prev, lag, done):
                step(u, prev, lag)
                if done is not None:
                    logits(done)
                if lag is not None and 3 <= lag.b < B-1:
                    keep_warm(1, bank[7])

            produce(ln2_units()[EARLY])
            for i, (_, *units) in enumerate(ln2_steps()[EARLY:], start=EARLY):
                step2(ln2_units()[i + 1] if i + 1 < B else None, *units)

            keep_warm(5)
            pe.wait_ge(s_ht, B)
            pe.wait_ge(s_d, CHOSEN_STEP)
            pe.matmul(bank[0][:, 0:EXPERTS * TB], before[:, :], chosen, start=True, stop=True)
            pe.matmul(bank[1][:, 0:EXPERTS * TB], ones[:, 0:P], chosen, start=True, stop=True).then_inc(s_rank, 1)
            keep_warm(9)
            for t in range(TB):
                if t % PLACES == 0:
                    pe.wait_ge(s_d, PLACE_STEP + t // PLACES)
                    pe.wait_ge(s_hg, 2 * (t // PLACES + 1))
                mm = pe.matmul(bank[7][:, 0:3 * SLOT_BLOCKS], place[:, t, :], held[:, t, :, :].rearrange("p a k -> p (a k)"),
                               start=(t == 0), stop=(t == TB - 1))
            mm.then_inc(s_slots, 1)
            keep_warm(4)
            pe.wait_ge(s_d, DISPATCH_STEPS)

            def block_step(blk, first, last):
                x, w, h, y = blk(2), blk(1), blk(0), blk(-1)
                e_w = block_expert(pe, w) if first else ahead[0]
                if x is not None:
                    pe.wait_ge(s_xh[x.slot], 16 * (x.turn + 1))
                    wait(pe, s_xbt, x.i - 1)
                    pe.transpose(bank[x.side][:, 0:P], xh[:, x.slot, 0:C], ident[:, :]).then_inc(s_xbps, 1)
                if w is not None:
                    pe.wait_ge(s_xbt, w.i + 1)
                    wait(pe, s_hb, w.i - 1)
                    pe.matmul(bank[2 + w.side], xbt[:, w.side, :], e1_sb[:, bass.ds(e_w * HID, HID)],
                              start=True, stop=True).then_inc(s_hps, 1)
                e_y = block_expert(pe, y)
                if h is not None:
                    pe.wait_ge(s_hb, h.i + 1)
                    wait(pe, s_hbt, h.i - 1)
                    for n in range(HID // P):
                        mm = pe.transpose(bank[4 + h.side][:, n * P:(n + 1) * P],
                                          hb[:, h.side, n * P:(n + 1) * P], ident[:, :])
                    mm.then_inc(s_htps, 1)
                if y is not None:
                    pe.wait_ge(s_hbt, y.i + 1)
                    wait(pe, s_yb, y.i - 1)
                    for n in range(HID // P):
                        mm = pe.matmul(bank[6 + y.side][:, 0:C], hbt[:, y.side, n * P:(n + 1) * P],
                                       e2_sb[:, bass.ds(e_y * HID + n * C, C)],
                                       start=(n == 0), stop=(n == HID // P - 1))
                    mm.then_inc(s_yps, 1)
                ahead[0] = None if last else block_expert(pe, x)

            ahead = [None]
            walk_blocks(pe, block_step)

        @block.vector
        def _(dve):
            dve.wait_ge(s_const, CONSTS)
            dve.wait_ge(s_lde, 16 * EMB_LOADS)

            def one_hot(b):
                dve.wait_ge(s_tok[b], 16)
                t = tok[:, b, :]
                wait(dve, s_y, b - 1)
                dve.tensor_scalar(onehot[:, b % 2, :], t[0:VOCAB, :], iota_p[0:VOCAB, 0:1], None,
                                  ALU.is_equal).then_inc(s_hot, 1)

            def source(u):
                if u.kind == "ln2":
                    return htok[:, u.b * NB:(u.b + 1) * NB, :]
                return Y[u.slot].rearrange("p (n c) -> p n c", c=C)

            def statistics(u):
                if u.kind == "ln2":
                    dve.wait_ge(s_ht, u.b + 1)
                else:
                    dve.wait_ge(s_y, u.n + 1)
                src = source(u)
                for j in range(NB):
                    ins = dve.bn_stats(bns[:, u.slot, j, :], src[:, j, :])
                ins.then_inc(s_bn, 1)

            def invert_root(u):
                dve.wait_ge(s_std, u.n + 1)
                dve.reciprocal(rstd[:, u.slot, :], std[:, u.slot, :]).then_inc(s_rstd, 1)

            def aggregate(u):
                if u.kind == "ln2" and u.b >= 4:
                    dve.wait_ge(s_xnp, u.b - 3)
                for j in range(NB):
                    ins = dve.bn_aggr(mv[:, u.slot, j, :], bns[:, u.slot, j, :])
                if u.kind == "ln1":
                    ins.then_inc(s_ag, 1)
                    dve.wait_ge(s_ag, u.b + 1)
                    var = mv[:, u.slot, :, 1]
                    ins = dve.tensor_scalar(var, var, VAR_FLOOR, None, ALU.max)
                ins.then_inc(s_var, 1)

            def normalise(u):
                dve.wait_ge(s_rstd, u.n + 1)
                if u.kind != "ln2":
                    wait(dve, s_t, u.n - 1)
                for j in range(NB - POOL_BLOCKS if u.kind == "ln2" else NB):
                    src = source(u)[:, j, :]
                    dst = xf[:, u.b * NB + j, :] if u.kind == "ln2" else xn[:, u.side, j, :]
                    ins = dve.tensor_scalar(dst, src, mv[:, u.slot, j, 0:1], rstd[:, u.slot, j:j + 1],
                                            ALU.subtract, ALU.mult)
                ins.then_inc(s_xn, 1)

            def step(u, prev, _):
                if u is not None and u.kind == "embed" and u.b + 1 < B:
                    one_hot(u.b + 1)
                if u is not None and u.kind == "embed" and u.b == 1:
                    dve.wait_ge(s_colps, 1)
                    dve.tensor_copy(cols[:, :], T[1][:, 0:ROWS]).then_inc(s_col, 1)
                if u is not None:
                    statistics(u)
                    dve.wait_ge(s_bn, u.n + 1)
                if prev is not None:
                    invert_root(prev)
                if u is not None:
                    aggregate(u)
                if prev is not None:
                    normalise(prev)

            one_hot(0)
            walk(dve, step)

            dve.wait_ge(s_ldr, 16 * REST_LOADS)
            dve.wait_ge(s_scaled, 3)

            def add_v_bias(b, j):
                dve.wait_ge(s_vps, NB * b + j + 1)
                dve.tensor_tensor(vv[:, j, :], ps_s[j], bv_rep[:, :], ALU.add).then_inc(s_v, 1)

            def clip_exp(m):
                dve.wait_ge(s_e, m + 1)
                dve.tensor_scalar(expa, expa, 1.0 / DECAY_FLOOR - 1.0, None, ALU.min).then_inc(s_em, 1)

            def sums(m):
                dve.wait_ge(s_sp, m + 1)
                wait(dve, s_dec, m)
                dve.tensor_tensor_scan(cum, ones[:, :], soft, 0.0, ALU.mult, ALU.add).then_inc(s_scan, 1)

            def clip_sums(m):
                dve.wait_ge(s_scan, m + 1)
                wait(dve, s_inv, m)
                dve.tensor_scalar(cumc, cum, float(-np.log(INV_FLOOR)), None, ALU.min).then_inc(s_cc, 1)

            def decayed(m, pair):
                dve.wait_ge(s_kps, m + 1)
                dve.wait_ge(s_inv, m + 1)
                dve.scalar_tensor_tensor(out=kd[:, pair % 2, :], in0=ps_ak, scalar=cols[:, R_BK + pair:R_BK + pair + 1],
                                         in1=inv_decay, op0=ALU.add, op1=ALU.mult).then_inc(s_k, 1)
                dve.wait_ge(s_qps, m + 1)
                dve.wait_ge(s_dec, m + 1)
                dve.scalar_tensor_tensor(out=qd[:, pair % 2, :], in0=ps_q, scalar=bqs[:, pair:pair + 1],
                                         in1=decay, op0=ALU.add, op1=ALU.mult).then_inc(s_q, 1)

            def mask(m, c):
                dve.wait_ge(s_sps, NB * m + c + 1)
                dve.tensor_tensor(probs[:, c % 2, :, :], psum[:, 4 + c % 2 * 2:6 + c % 2 * 2, 0:P],
                                  causal[:, :].unsqueeze(1).to_broadcast([P, 2, P]), ALU.mult).then_inc(s_p, 1)

            def take_keys(m):
                dve.wait_ge(s_knps, m + 1)
                dve.tensor_copy(kn[:, :, :], ps_kso[:, 0:(NB - 1) * P].rearrange("p (n c) -> p n c", c=P)).then_inc(s_kn, 1)

            def add_state(m, c):
                dve.wait_ge(s_stps, (NB - 1) * m + c + 1)
                if c:
                    dve.wait_ge(s_st, (NB - 1) * m + c)
                for h in range(2):
                    r = slice(h * DH, (h + 1) * DH)
                    new = ps_kso[r, 3 * P + h * DH:3 * P + (h + 1) * DH]
                    if c == 0:
                        ins = dve.tensor_copy(state[r, 0, r], new)
                    else:
                        ins = dve.tensor_tensor(state[r, c % 2, r], new, state[r, (c - 1) % 2, r], ALU.add)
                ins.then_inc(s_st, 1)

            def add_attention(b):
                dve.wait_ge(s_ops, b + 1)
                row = res[:, bass.ds(b, 1), 1:S + 1].rearrange("p a s -> p (a s)")
                dve.scalar_tensor_tensor(out=row, in0=ps_out, scalar=cols[:, R_BOUT:R_BOUT + 1], in1=row,
                                         op0=ALU.add, op1=ALU.add).then_inc(s_h, 1)

            def attend(m, b, pair, last):
                more = not (last and pair == PAIRS - 1)
                if more:
                    clip_exp(m + 1)
                take_keys(m)
                mask(m, 0)
                mask(m, 1)
                if more:
                    sums(m + 1)
                    clip_sums(m + 1)
                add_state(m, 0)
                mask(m, 2)
                add_state(m, 1)
                if more:
                    decayed(m + 1, (pair + 1) % PAIRS)
                mask(m, 3)
                add_state(m, 2)
                if pair == PAIRS - 1:
                    if not last:
                        add_v_bias(b + 1, 0)
                        add_v_bias(b + 1, 1)
                    if not last:
                        add_attention(b)
                        add_v_bias(b + 1, 2)
                        add_v_bias(b + 1, 3)

            clip_exp(0)
            add_v_bias(0, 0)
            add_v_bias(0, 1)
            sums(0)
            clip_sums(0)
            add_v_bias(0, 2)
            add_v_bias(0, 3)
            decayed(0, 0)
            with dve.Fori(0, B - 1) as b:
                for pair in range(PAIRS):
                    attend(PAIRS * b + pair, b, pair, False)
            for pair in range(PAIRS):
                attend(PAIRS * (B - 1) + pair, B - 1, pair, True)

            for i, (u, prev, lag, _) in enumerate(ln2_steps()):
                if i == EARLY:
                    add_attention(B - 1)
                step(u, prev, lag)
            dve.wait_ge(s_rows, 16 * (2 * B + 1))
            dve.wait_ge(s_ids, 1)

            steps = [0]

            def then(ins):
                steps[0] += 1
                ins.then_inc(s_d, 1)
                dve.wait_ge(s_d, steps[0])

            def by_block(i):
                return small[:, i, :].rearrange("p (t e) -> p t e", e=EXPERTS)

            def by_expert(i):
                return small[:, i, :].rearrange("p (e t) -> p e t", e=EXPERTS)

            rank8 = ramps[:, 0:EXPERTS]
            full = ramps[:, EXPERTS:EXPERTS + TB]
            number = ramps[:, EXPERTS + TB:EXPERTS + TB + SLOT_BLOCKS]
            in_block = ramps[:, EXPERTS + TB + SLOT_BLOCKS:RAMPS]
            slot_hi, slot_lo = small[:, 0, 0:TB], small[:, 0, TB:2 * TB]
            first8 = small[:, 1, TB:2 * TB]
            slot_f = small[:, 1, 2 * TB:3 * TB]
            count, blocks = small[:, 8, 0:8], small[:, 8, 8:16]
            end_block, start_block, shift = small[:, 8, 16:24], small[:, 8, 24:32], small[:, 8, 32:40]
            wide = [P, TB, EXPERTS]
            dve.wait_ge(s_lg, B)
            then(dve.tensor_tensor(by_block(0), bank[6][:, 0:TB * EXPERTS].rearrange("p (t e) -> p t e", e=EXPERTS),
                                   br_rep[:, :].unsqueeze(1).to_broadcast(wide), ALU.add))
            then(dve.tensor_reduce(top, by_block(0), AX.X, ALU.max))
            then(dve.tensor_tensor(by_block(2), by_block(0), top.unsqueeze(2).to_broadcast(wide), ALU.is_ge))
            then(dve.tensor_tensor(by_block(3), by_block(2), rank8.unsqueeze(1).to_broadcast(wide), ALU.mult))
            then(dve.tensor_reduce(first8, by_block(3), AX.X, ALU.max))
            then(dve.tensor_copy(by_expert(5), rank8.unsqueeze(2).to_broadcast([P, EXPERTS, TB])))
            then(dve.tensor_tensor(by_expert(4), by_expert(5), first8.unsqueeze(1).to_broadcast([P, EXPERTS, TB]),
                                   ALU.is_equal))
            then(dve.tensor_tensor(gate_arg, top, top, ALU.subtract))
            dve.wait_ge(s_gexp, 1)
            then(dve.reciprocal(gate_inv, gate_exp))
            then(dve.tensor_tensor(gate, gate_exp, gate_inv, ALU.mult))
            then(dve.tensor_copy(gate_parts[:, 0, :], gate))
            then(dve.tensor_tensor(gate_parts[:, 1, :], gate, gate_parts[:, 0, :], ALU.subtract))
            dve.wait_ge(s_rank, 1)
            then(dve.tensor_copy(small[:, 5, :], bank[1][:, 0:EXPERTS * TB]))
            then(dve.tensor_tensor_scan(small[:, 6, :], ones[:, 0:EXPERTS * TB], small[:, 5, :], 0.0, ALU.mult, ALU.add))
            then(dve.tensor_tensor(small[:, 7, :], small[:, 6, :], small[:, 5, :], ALU.subtract))
            then(dve.tensor_tensor(count, by_expert(6)[:, :, TB - 1], by_expert(7)[:, :, 0], ALU.subtract))
            then(dve.tensor_tensor(by_expert(9), count.unsqueeze(2).to_broadcast([P, EXPERTS, TB]),
                                   full.unsqueeze(1).to_broadcast([P, EXPERTS, TB]), ALU.is_gt))
            then(dve.tensor_reduce(blocks, by_expert(9), AX.X, ALU.add))
            then(dve.tensor_tensor_scan(end_block, ones[:, 0:EXPERTS], blocks, 0.0, ALU.mult, ALU.add))
            then(dve.tensor_tensor(start_block, end_block, blocks, ALU.subtract))
            then(dve.scalar_tensor_tensor(out=shift, in0=start_block, scalar=float(P), in1=by_expert(7)[:, :, 0],
                                          op0=ALU.mult, op1=ALU.subtract))
            then(dve.tensor_tensor(by_expert(10), by_expert(7), shift.unsqueeze(2).to_broadcast([P, EXPERTS, TB]),
                                   ALU.add))
            then(dve.tensor_tensor(small[:, 11, :], bank[0][:, 0:EXPERTS * TB], small[:, 10, :], ALU.add))
            then(dve.tensor_tensor(small[:, 10, :], small[:, 11, :], chosen, ALU.mult))
            then(dve.tensor_reduce(slot_f, small[:, 10, :].rearrange("p (e t) -> p t e", e=EXPERTS), AX.X, ALU.add))
            then(dve.tensor_copy(slot_u[:, 0, :], slot_f))
            then(dve.tensor_scalar(slot_u[:, 1, :], slot_u[:, 0, :], P.bit_length() - 1, None, ALU.logical_shift_right))
            then(dve.tensor_copy(slot_hi, slot_u[:, 1, :]))
            then(dve.scalar_tensor_tensor(out=slot_lo, in0=slot_hi, scalar=-float(P), in1=slot_f, op0=ALU.mult, op1=ALU.add))
            in_k = [P, TB, SLOT_BLOCKS]
            then(dve.tensor_tensor(in_slot_block, number.unsqueeze(1).to_broadcast(in_k),
                                   slot_hi.unsqueeze(2).to_broadcast(in_k), ALU.is_equal))
            assert steps[0] == BLOCK_STEP
            then(dve.tensor_tensor(held[:, :, 0, :], in_slot_block, ids[:, :].unsqueeze(2).to_broadcast(in_k), ALU.mult))
            for t in range(0, TB, PLACES):
                wide_place = [P, PLACES, P]
                ins = dve.tensor_tensor(place[:, t:t + PLACES, :], in_block.unsqueeze(1).to_broadcast(wide_place),
                                        slot_lo[:, t:t + PLACES].unsqueeze(2).to_broadcast(wide_place), ALU.is_equal)
                steps[0] += 1
                ins.then_inc(s_d, 1)
                if t == 0:
                    assert steps[0] == PLACE_STEP
            ended = small[:, 2:4, :].rearrange("p a b -> p (a b)")[:, 0:SLOT_BLOCKS * (EXPERTS - 1)]
            ended = ended.rearrange("p (i e) -> p i e", e=EXPERTS - 1)
            narrow = [P, SLOT_BLOCKS, EXPERTS - 1]
            then(dve.tensor_tensor(ended, number.unsqueeze(2).to_broadcast(narrow),
                                   end_block[:, 0:EXPERTS - 1].unsqueeze(1).to_broadcast(narrow), ALU.is_ge))
            then(dve.tensor_reduce(small[:, 9, 0:SLOT_BLOCKS], ended, AX.X, ALU.add))
            then(dve.tensor_copy(blk_e[:, :], small[:, 9, 0:SLOT_BLOCKS]))
            dve.wait_ge(s_slots, 1)
            then(dve.tensor_copy(slot_row[:, 0:3, :], bank[7][:, 0:3 * SLOT_BLOCKS].rearrange("p (a k) -> p a k", a=3)))
            then(dve.tensor_scalar(slot_row[:, 3, :], slot_row[:, 0, :], 0.0, float(B * S + 1), ALU.is_equal, ALU.mult))
            then(dve.tensor_tensor(slot_row[:, 0, :], slot_row[:, 0, :], slot_row[:, 3, :], ALU.add))
            assert steps[0] == DISPATCH_STEPS

            def block_step(blk, first, last):
                new, w, y = blk(AHEAD), blk(1), blk(-1)
                e_w = block_expert(dve, w) if first else ahead[0]
                if new is not None:
                    wait(dve, s_xh[new.slot], 16 * new.turn)
                    dve.tensor_scalar(idx[:, 0, new.slot:new.slot + 1], slot_row[:, 0, bass.ds(new.i, 1)], -1.0, None,
                                      ALU.add).then_inc(s_idx, 1)
                if w is not None and isinstance(w.i, int) and w.i == 0:
                    dve.tensor_tensor(slot_row[:, 1, :], slot_row[:, 1, :], slot_row[:, 2, :], ALU.add).then_inc(s_gcol, 1)
                if w is not None:
                    dve.wait_ge(s_hps, w.i + 1)
                    wait(dve, s_htps, w.i - 1)
                    dve.tensor_tensor(hb[:, w.side, :], bank[2 + w.side], eb1_rep[:, bass.ds(e_w * HID, HID)],
                                      ALU.add).then_inc(s_hb, 1)
                e_y = block_expert(dve, y)
                if y is not None:
                    if isinstance(y.i, int) and y.i == 0:
                        dve.wait_ge(s_gcol, 1)
                    dve.wait_ge(s_yps, y.i + 1)
                    dve.tensor_tensor(yb[:, y.side, :], bank[6 + y.side][:, 0:C],
                                      eb2_rep[:, bass.ds(e_y * C, C)], ALU.add).then_inc(s_yb, 1)
                    wait(dve, s_sc[y.slot], 16 * y.turn)
                    dve.tensor_scalar(idx[:, 1, y.slot:y.slot + 1], slot_row[:, 0, bass.ds(y.i, 1)], -1.0, None,
                                      ALU.add)
                    dve.wait_ge(s_yb, y.i + 1)
                    dve.scalar_tensor_tensor(out=ob[:, y.slot, :], in0=yb[:, y.side, :],
                                             scalar=slot_row[:, 1, bass.ds(y.i, 1)], in1=xh[:, y.slot, C:2 * C],
                                             op0=ALU.mult, op1=ALU.add).then_inc(s_ob, 1)
                ahead[0] = None if last else block_expert(dve, blk(2))

            ahead = [None]
            walk_blocks(dve, block_step)


_INS = ["x", "L0_tok_emb", "L0_tok_ln0_g", "L0_tok_ln0_b", "L0_tok_W1", "L0_tok_g1", "L0_tok_b1", "L0_tok_W2",
        "L0_tok_g2", "L0_tok_b2", "L0_attn_gamma", "L0_attn_w_qkv", "L0_attn_b_qkv", "L0_attn_w_a", "L0_attn_b_a",
        "L0_attn_w_out", "L0_attn_b_out", "L0_ffn_Wr", "L0_ffn_br", "L0_ffn_W1", "L0_ffn_b1", "L0_ffn_W2",
        "L0_ffn_b2"]


def _constants():
    f = np.float32
    pos = np.arange(S - 1, -1, -1, dtype=f)
    inv_freq = f(1.0) / np.power(f(10000.0), np.arange(0.0, C, 2.0, dtype=f) / f(C))
    arg = pos[:, None] * inv_freq[None, :]
    pe = np.concatenate([np.sin(arg), np.cos(arg)], axis=-1).astype(f)
    at = np.arange(P)
    ramps = np.concatenate([EXPERTS - np.arange(EXPERTS), P * np.arange(TB), np.arange(SLOT_BLOCKS),
                            np.arange(P)]).astype(f)
    return {"pe": pe, "identity": np.eye(P, dtype=f), "causal": (at[:, None] <= at[None, :]).astype(f),
            "before": (at[:, None] < at[None, :]).astype(f), "ramps": ramps}


def kernel(**inputs):
    import concourse.bacc as bacc
    from concourse.bass_utils import run_bass_kernel_spmd

    nc = bacc.Bacc("TRN2", target_bir_lowering=False, num_devices=1)
    arrays, args = {}, []
    given = {name: np.ascontiguousarray(inputs[name]) for name in _INS}
    for name, a in {**given, **_constants()}.items():
        arrays[f"in_{name}"] = a
        args.append(nc.dram_tensor(f"in_{name}", a.shape, mybir.dt.from_np(a.dtype), kind="ExternalInput").ap())
    out = nc.dram_tensor("out", (B, S, C), F32, kind="ExternalOutput").ap()
    tower(nc, *args, out)
    r = run_bass_kernel_spmd(nc, [arrays], core_ids=[0])
    return r.results[0]["out"]
```
